# Optimizing a Trainium2 kernel written in Bass

```python
import numpy as np
import jax
import jax.numpy as jnp

def _softmax(x, axis=-1):
    return jax.nn.softmax(x, axis=axis)

def _gelu(x):
    return jax.nn.gelu(x, approximate=True)

def _silu(x):
    return jax.nn.silu(x)

def _sigmoid(x):
    return jax.nn.sigmoid(x)

def _layernorm(x, axis=-1, eps=1e-05):
    m = jnp.mean(x, axis=axis, keepdims=True)
    v = jnp.var(x, axis=axis, keepdims=True)
    return (x - m) / jnp.sqrt(v + eps)

def _scatter_add(tgt, idx, src, axis=0):
    return tgt.at[idx].add(src)

def _segment_sum(src, seg, n):
    return jax.ops.segment_sum(src, seg, n)
kernel_name = 'mk_seq_postln_d1_jaxref_r4_00c25b'

def setup_inputs(seed: int=0):
    np.random.seed(seed)
    _w = jnp.asarray

    def _L0_attn_setup():
        import math
        import jax, jax.numpy as jnp
        import numpy as np
        EMBED_DIM = 256
        NUM_HEADS = 16
        HEAD_DIM = EMBED_DIM // NUM_HEADS
        NUM_BUCKETS = 80
        MAX_DISTANCE = 200

        def _relative_position_bucket(q_len, k_len):
            ctx = jnp.arange(q_len, dtype=jnp.int32)[:, None]
            mem = jnp.arange(k_len, dtype=jnp.int32)[None, :]
            rel = mem - ctx
            nb = NUM_BUCKETS // 2
            buckets = (rel > 0).astype(jnp.int32) * nb
            rel_abs = jnp.abs(rel)
            max_exact = nb // 2
            is_small = rel_abs < max_exact
            large = jnp.log(jnp.maximum(rel_abs, 1).astype(jnp.float32) / max_exact) / math.log(MAX_DISTANCE / max_exact) * (nb - max_exact)
            large = (max_exact + large).astype(jnp.int32)
            large = jnp.minimum(large, nb - 1)
            return buckets + jnp.where(is_small, rel_abs, large)
        key = jax.random.key(seed)
        ks = jax.random.split(key, 12)
        B, N, E = (4, 256, EMBED_DIM)
        s = 0.02
        inp = {'hidden_states': jax.random.normal(ks[0], (B, N, E), jnp.float32), 'Wq': jax.random.normal(ks[1], (E, E), jnp.float32) * s, 'bq': jnp.zeros((E,), jnp.float32), 'Wk': jax.random.normal(ks[2], (E, E), jnp.float32) * s, 'bk': jnp.zeros((E,), jnp.float32), 'Wv': jax.random.normal(ks[3], (E, E), jnp.float32) * s, 'bv': jnp.zeros((E,), jnp.float32), 'Wo': jax.random.normal(ks[4], (E, E), jnp.float32) * s, 'bo': jnp.zeros((E,), jnp.float32), 'gru_const': jnp.ones((1, NUM_HEADS, 1, 1), jnp.float32), 'gru_W': jax.random.normal(ks[5], (8, HEAD_DIM), jnp.float32) * s, 'gru_b': jnp.zeros((8,), jnp.float32), 'rel_embed': jax.random.normal(ks[6], (NUM_BUCKETS, NUM_HEADS), jnp.float32) * s}
        return inp
    _L0_attn_in = _L0_attn_setup()

    def _L0_ffn_setup():
        import jax, jax.numpy as jnp
        import numpy as np
        E = 8
        TOP_K = 2
        CAP_FACTOR = 1.25
        MIN_CAP = 4
        SCORE_SCALE = 1.0

        def _ffn(x, w1, b1, w2, b2):
            return jax.nn.gelu(x @ w1 + b1, approximate=False) @ w2 + b2
        key = jax.random.key(seed)
        ks = jax.random.split(key, 6)
        B, S, D, I = (4, 512, 256, 1024)
        std = 0.02
        return {'x': jax.random.normal(ks[0], (B, S, D), jnp.float32), 'Wr': jax.random.normal(ks[1], (E, D), jnp.float32) * std, 'W1': jax.random.normal(ks[2], (E, D, I), jnp.float32) * std, 'b1': jnp.zeros((E, I), jnp.float32), 'W2': jax.random.normal(ks[3], (E, I, D), jnp.float32) * std, 'b2': jnp.zeros((E, D), jnp.float32), 'fw1': jax.random.normal(ks[4], (D, I), jnp.float32) * std, 'fb1': jnp.zeros((I,), jnp.float32), 'fw2': jax.random.normal(ks[5], (I, D), jnp.float32) * std, 'fb2': jnp.zeros((D,), jnp.float32)}
    _L0_ffn_in = _L0_ffn_setup()
    _d = {'L0_attn_hidden_states': _L0_attn_in['hidden_states'], 'L0_attn_Wq': _L0_attn_in['Wq'], 'L0_attn_bq': _L0_attn_in['bq'], 'L0_attn_Wk': _L0_attn_in['Wk'], 'L0_attn_bk': _L0_attn_in['bk'], 'L0_attn_Wv': _L0_attn_in['Wv'], 'L0_attn_bv': _L0_attn_in['bv'], 'L0_attn_Wo': _L0_attn_in['Wo'], 'L0_attn_bo': _L0_attn_in['bo'], 'L0_attn_gru_const': _L0_attn_in['gru_const'], 'L0_attn_gru_W': _L0_attn_in['gru_W'], 'L0_attn_gru_b': _L0_attn_in['gru_b'], 'L0_attn_rel_embed': _L0_attn_in['rel_embed'], 'L0_ffn_Wr': _L0_ffn_in['Wr'], 'L0_ffn_W1': _L0_ffn_in['W1'], 'L0_ffn_b1': _L0_ffn_in['b1'], 'L0_ffn_W2': _L0_ffn_in['W2'], 'L0_ffn_b2': _L0_ffn_in['b2'], 'L0_ffn_fw1': _L0_ffn_in['fw1'], 'L0_ffn_fb1': _L0_ffn_in['fb1'], 'L0_ffn_fw2': _L0_ffn_in['fw2'], 'L0_ffn_fb2': _L0_ffn_in['fb2']}
    _x0 = _d['L0_attn_hidden_states']
    _d['L0_attn_hidden_states'] = jax.random.normal(jax.random.fold_in(jax.random.key(seed), 1), (8, 1024, 256), dtype=_x0.dtype)
    del _x0
    return _d

def reference(L0_attn_hidden_states, L0_attn_Wq, L0_attn_bq, L0_attn_Wk, L0_attn_bk, L0_attn_Wv, L0_attn_bv, L0_attn_Wo, L0_attn_bo, L0_attn_gru_const, L0_attn_gru_W, L0_attn_gru_b, L0_attn_rel_embed, L0_ffn_Wr, L0_ffn_W1, L0_ffn_b1, L0_ffn_W2, L0_ffn_b2, L0_ffn_fw1, L0_ffn_fb1, L0_ffn_fw2, L0_ffn_fb2):

    def _L0_attn_ref(hidden_states, Wq, bq, Wk, bk, Wv, bv, Wo, bo, gru_const, gru_W, gru_b, rel_embed):
        import math
        import jax, jax.numpy as jnp
        import numpy as np
        EMBED_DIM = 256
        NUM_HEADS = 16
        HEAD_DIM = EMBED_DIM // NUM_HEADS
        NUM_BUCKETS = 80
        MAX_DISTANCE = 200

        def _relative_position_bucket(q_len, k_len):
            ctx = jnp.arange(q_len, dtype=jnp.int32)[:, None]
            mem = jnp.arange(k_len, dtype=jnp.int32)[None, :]
            rel = mem - ctx
            nb = NUM_BUCKETS // 2
            buckets = (rel > 0).astype(jnp.int32) * nb
            rel_abs = jnp.abs(rel)
            max_exact = nb // 2
            is_small = rel_abs < max_exact
            large = jnp.log(jnp.maximum(rel_abs, 1).astype(jnp.float32) / max_exact) / math.log(MAX_DISTANCE / max_exact) * (nb - max_exact)
            large = (max_exact + large).astype(jnp.int32)
            large = jnp.minimum(large, nb - 1)
            return buckets + jnp.where(is_small, rel_abs, large)
        B, N, E = hidden_states.shape
        H, D = (NUM_HEADS, HEAD_DIM)

        def split_heads(x):
            return x.reshape(B, N, H, D).transpose(0, 2, 1, 3)
        q = split_heads(hidden_states @ Wq.T + bq)
        k = split_heads(hidden_states @ Wk.T + bk)
        v = split_heads(hidden_states @ Wv.T + bv)
        buckets = _relative_position_bucket(N, N)
        pos_bias = jnp.transpose(rel_embed[buckets], (2, 0, 1))
        ghs = split_heads(hidden_states)
        proj = ghs @ gru_W.T + gru_b
        proj = proj.reshape(B, H, N, 2, 4).sum(-1)
        gates = jax.nn.sigmoid(proj)
        gate_a, gate_b = (gates[..., 0:1], gates[..., 1:2])
        gate_out = gate_a * (gate_b * gru_const - 1.0) + 2.0
        gated_bias = gate_out * pos_bias[None]
        scale = 1.0 / math.sqrt(D)
        scores = jnp.einsum('bhid,bhjd->bhij', q, k) * scale + gated_bias
        attn = jax.nn.softmax(scores, axis=-1)
        out = jnp.einsum('bhij,bhjd->bhid', attn, v)
        out = out.transpose(0, 2, 1, 3).reshape(B, N, E)
        return out @ Wo.T + bo

    def _L0_ffn_ref(x, Wr, W1, b1, W2, b2, fw1, fb1, fw2, fb2):
        import jax, jax.numpy as jnp
        import numpy as np
        E = 8
        TOP_K = 2
        CAP_FACTOR = 1.25
        MIN_CAP = 4
        SCORE_SCALE = 1.0

        def _ffn(x, w1, b1, w2, b2):
            return jax.nn.gelu(x @ w1 + b1, approximate=False) @ w2 + b2
        B, S, D = x.shape
        T = B * S
        x_flat = x.reshape(T, D)
        logits = x_flat @ Wr.T * SCORE_SCALE
        probs = jax.nn.softmax(logits, axis=-1)
        topk_scores, topk_experts = jax.lax.top_k(probs, TOP_K)
        topk_scores = topk_scores / jnp.clip(topk_scores.sum(-1, keepdims=True), 1e-09, None)
        cap = max(int(CAP_FACTOR * (T * TOP_K / E)), MIN_CAP)
        y_fb = _ffn(x_flat, fw1, fb1, fw2, fb2)
        y_flat = jnp.zeros_like(x_flat)
        fallback = jnp.zeros((T,), bool)
        tok_ids = jnp.arange(T, dtype=jnp.int32)
        for e in range(E):
            match = topk_experts == e
            elig = match.any(-1) & ~fallback
            pos = jnp.cumsum(elig) - 1
            kept = elig & (pos < cap)
            overflow = elig & (pos >= cap)
            slot = jnp.where(kept, pos, cap)
            buf = jnp.zeros((cap + 1,), jnp.int32).at[slot].set(tok_ids)
            vmask = jnp.zeros((cap + 1,), bool).at[slot].set(kept)
            idx = buf[:cap]
            valid = vmask[:cap]
            x_e = x_flat[idx]
            y_e = _ffn(x_e, W1[e], b1[e], W2[e], b2[e])
            w_tok = (topk_scores * match).sum(-1)
            w = jnp.where(valid, w_tok[idx], 0.0)
            y_flat = y_flat.at[idx].add(y_e * w[:, None])
            y_flat = jnp.where(overflow[:, None], y_fb, y_flat)
            fallback = fallback | overflow
        return y_flat.reshape(B, S, D)
    x = L0_attn_hidden_states
    x = _layernorm(x + _L0_attn_ref(x, L0_attn_Wq, L0_attn_bq, L0_attn_Wk, L0_attn_bk, L0_attn_Wv, L0_attn_bv, L0_attn_Wo, L0_attn_bo, L0_attn_gru_const, L0_attn_gru_W, L0_attn_gru_b, L0_attn_rel_embed), axis=-1)
    x = _layernorm(x + _L0_ffn_ref(x, L0_ffn_Wr, L0_ffn_W1, L0_ffn_b1, L0_ffn_W2, L0_ffn_b2, L0_ffn_fw1, L0_ffn_fb1, L0_ffn_fw2, L0_ffn_fb2), axis=-1)
    return x

_drawn_inputs = setup_inputs


def setup_inputs(seed=0):
    import zlib

    import numpy as np

    out = dict(_drawn_inputs(seed))
    spreads = {'L0_attn_bq': (0.0, 0.8),
     'L0_attn_bk': (0.0, 2.0),
     'L0_attn_bv': (0.0, 0.1),
     'L0_attn_bo': (0.0, 0.1),
     'L0_attn_gru_const': (1.0, 0.6),
     'L0_attn_gru_b': (0.0, 2.0),
     'L0_ffn_b1': (0.0, 0.308),
     'L0_ffn_b2': (0.0, 0.1),
     'L0_ffn_fb1': (0.0, 0.8),
     'L0_ffn_fb2': (0.0, 2.0)}
    factors = {'L0_attn_Wq': 8.0,
     'L0_attn_Wk': 8.0,
     'L0_attn_Wv': 7.167,
     'L0_attn_gru_W': 113.961,
     'L0_attn_rel_embed': 8.0,
     'L0_ffn_fw1': 3.67,
     'L0_ffn_fw2': 3.457}
    for name, (base, spread) in spreads.items():
        noise = np.random.default_rng([zlib.crc32(name.encode()), seed]).standard_normal(out[name].shape)
        drawn = base * np.exp(spread * noise) if base else spread * noise
        out[name] = jnp.asarray(drawn.astype(out[name].dtype))
    for name, factor in factors.items():
        out[name] = (out[name] * factor).astype(out[name].dtype)
    return out
```

```python
import math
from contextlib import ExitStack

import numpy as np

import concourse.bass as bass
from concourse import mybir

P = 128
F32 = mybir.dt.float32
BF16 = mybir.dt.bfloat16
I32 = mybir.dt.int32
U32 = mybir.dt.uint32
ALU = mybir.AluOpType
ACT = mybir.ActivationFunctionType
AX = mybir.AxisListType

B, N, E = 8, 1024, 256
H, D = 16, 16
T = B * N
EC = E // P
HQ = 4
NI = N // P
NB, MAXD = 80, 200
NEG, POS = NB // 2 - 1, NB - 1
EPS = 1e-5
NE, TOPK, HID = 8, 2, 1024
CAP = max(int(1.25 * (T * TOPK / NE)), 4)
TT = T // P
RT = 512
SLOTS = NE * CAP
ROWS = SLOTS + T
HC = HID // P
ZW = 2048
NZ = SLOTS * E // P // ZW
PIECES_Q = (0, 0, 1, 0, 2, 1)
PIECES_K = (0, 1, 0, 2, 0, 1)


def buckets(rel):
    nb = NB // 2
    a = np.abs(rel)
    big = np.log(np.maximum(a, 1).astype(np.float32) / np.float32(nb // 2)).astype(np.float32)
    big = (big / np.float32(math.log(MAXD / (nb // 2))) * np.float32(nb - nb // 2)).astype(np.float32)
    big = np.minimum((nb // 2 + big).astype(np.int32), nb - 1)
    return (rel > 0) * nb + np.where(a < nb // 2, a, big)


REACH = int(max(r for r in range(N) if buckets(np.array(-r)) != NEG)) + 1
BAND = 2 * REACH + P - 2
LINE = BAND + P - 1
LO = REACH - 1
assert LO < 2 * P and BAND - LO < 3 * P


def shape_constants():
    v = (np.arange(LINE) - LO - (P - 1))[::-1]
    c = {"c_onehot": (np.arange(NB)[:, None] == buckets(v)[None, :]).astype(np.float32)}
    hd, hj = np.arange(P) // D, np.arange(P) // NI
    c["c_mask_hj"] = np.stack([(hd[:, None] + 8 * k == hj[None, :]) for k in range(EC)]).astype(np.float32)
    c["c_mask_h"] = np.stack([(hd[:, None] + 8 * k == np.arange(H)[None, :]) for k in range(EC)]).astype(np.float32)
    j, i = (np.arange(P) % NI)[:, None], np.arange(NI)[None, :]
    c["c_far"] = np.stack([j - i <= -2, j - i >= 2]).astype(np.float32)
    ind = np.zeros((32, N), np.float32)
    for s in range(3):
        for b in range(NI):
            ind[8 * s + b, b * P:(b + 1) * P] = 1
    c["c_ind"] = ind
    c["c_ident"] = np.eye(P, dtype=np.float32)
    c["c_order"] = np.broadcast_to(np.arange(NE, dtype=np.float32) - NE, (P, NE))
    c["c_token"] = (SLOTS + np.arange(TT)[None, :] * P + np.arange(P)[:, None]).astype(np.float32)
    c["c_before"] = (np.arange(P)[:, None] < np.arange(P)[None, :]).astype(np.float32)
    return c


def layer(nc, a, out):
    es = ExitStack()

    def dram(name, shape, dt):
        return nc.dram_tensor(name, shape, dt, kind="Internal").ap()

    line_d = dram("line_d", [H, LINE], F32)
    slab_d = dram("slab_d", [P, H, BAND], F32)
    q_d = dram("q_d", [3, B, E, N], BF16)
    k_d = dram("k_d", [3, B, E, N], BF16)
    far_d = dram("far_d", [3, B, P, N], BF16)
    v_d = dram("v_d", [T, 2 * E], F32)
    gate_d = dram("gate_d", [B, P, P], F32)
    ot_d = dram("ot_d", [HQ, B, P, N], F32)
    xg_d = dram("xg_d", [ROWS, E], F32)
    yg_d = dram("yg_d", [ROWS, E], F32)

    with es:
        def sem(name):
            return es.enter_context(nc.semaphore(name))

        def keep(name, shape, dt=F32):
            return es.enter_context(nc.sbuf_tensor(name, shape, dt))

        ident = keep("ident", [P, P])
        gate_w = keep("gate_w", [P, EC, 2, P])
        gate_wt = keep("gate_wt", [P, EC, 2, H])
        gate_bs = keep("gate_bs", [P, 2])
        far_c = keep("far_c", [P, NI])
        logits = keep("logits", [P, TT, NE])
        slot_s = keep("slot_s", [P, TT, TOPK], U32)
        slot_g = keep("slot_g", [P, TT, TOPK], U32)
        wgt = keep("wgt", [P, TT, TOPK])
        zero = keep("zero", [P, ZW])
        zeroed = sem("zeroed")
        setup(nc, a, line_d, slab_d, xg_d, zeroed, zero, ident, gate_w, gate_wt, gate_bs, far_c)
        project(nc, a, q_d, k_d, far_d, v_d, gate_d, gate_w, gate_wt, gate_bs, far_c)
        attend(nc, a, q_d, k_d, far_d, v_d, gate_d, slab_d, ot_d, ident)
        merge(nc, a, ot_d, xg_d, ident, logits)
        route(nc, a, xg_d, zeroed, logits, slot_s, slot_g, wgt)
        ffn(nc, a, xg_d, yg_d, ident)
        combine(nc, a, xg_d, yg_d, slot_g, wgt, out)


def setup(nc, a, line_d, slab_d, xg_d, zeroed, zero, ident, gate_w, gate_wt, gate_bs, far_c):
    with ExitStack() as es:
        def sb(name, shape, dt=F32):
            return es.enter_context(nc.sbuf_tensor(name, shape, dt))

        def sem(name):
            return es.enter_context(nc.semaphore(name))

        onehot = sb("onehot", [NB, LINE])
        rel = sb("rel", [NB, H])
        line = sb("line", [H, LINE])
        falling = sb("falling", [P, H, BAND])
        slab = sb("slab", [P, H, BAND])
        ends = sb("ends", [P, 2, H])
        far_ends = sb("far_ends", [P, 2])
        far_mask = sb("far_mask", [P, 2, NI])
        far_t = sb("far_t", [P, NI])
        gw = sb("gw", [P, 2, 4])
        gb = sb("gb", [P, 2, 4])
        wsum = sb("wsum", [P, 2])
        mask_hj = sb("mask_hj", [P, EC, P])
        mask_h = sb("mask_h", [P, EC, H])
        pl = es.enter_context(nc.psum_tensor("pl", [H, 2, 512], F32))
        loaded = sem("loaded")
        line_ready, line_copied, line_stored = sem("line_ready"), sem("line_copied"), sem("line_stored")
        slab_loaded, slab_ready, slab_stored = sem("slab_loaded"), sem("slab_ready"), sem("slab_stored")
        zero_set, summed, far_part = sem("zero_set"), sem("summed"), sem("far_part")
        small = [(onehot[:], a["c_onehot"]), (rel[:], a["rel"]), (gw[:], a["gru_w"]), (gb[:], a["gru_b"]),
                 (mask_hj[:], a["c_mask_hj"].rearrange("k p n -> p k n")),
                 (mask_h[:], a["c_mask_h"].rearrange("k p n -> p k n")),
                 (far_mask[:], a["c_far"].rearrange("k p n -> p k n")),
                 (ends[:], a["ends"]), (far_ends[:], a["far_ends"]), (ident[:], a["c_ident"])]
        block = es.enter_context(nc.Block())

        @block.sync
        def _(sp):
            with nc.allow_non_contiguous_dma(reason="small constants, once"):
                for to, of in small:
                    sp.dma_start(to, of).then_inc(loaded, 16)
            sp.wait_ge(line_copied, 1)
            sp.dma_start(line_d, line[:]).then_inc(line_stored, 16)
            sp.wait_ge(line_stored, 16)
            for h in range(H):
                skew = bass.AP(line_d.tensor, h * LINE, [[1, P], [1, BAND]])
                sp.dma_start(falling[:, h, :], skew).then_inc(slab_loaded, 16)
            sp.wait_ge(slab_ready, 3)
            sp.dma_start(slab_d, slab[:]).then_inc(slab_stored, 16)
            sp.wait_ge(slab_stored, 16)

        @block.scalar
        def _(act):
            act.wait_ge(zero_set, 1)
            flat = xg_d[0:SLOTS, :].rearrange("(p r) e -> p (r e)", p=P)
            for c in range(NZ):
                act.dma_start(flat[:, c * ZW:(c + 1) * ZW], zero[:]).then_inc(zeroed, 16)

        @block.tensor
        def _(pe):
            pe.wait_ge(loaded, 16 * len(small))
            for c, (lo, hi) in enumerate(((0, 512), (512, LINE))):
                pe.matmul(pl[:, c, 0:hi - lo], rel[:], onehot[:, lo:hi], start=True, stop=True).then_inc(line_ready, 1)

        @block.vector
        def _(dve):
            dve.memset(zero[:], 0.0).then_inc(zero_set, 1)
            dve.wait_ge(loaded, 16 * len(small))
            dve.tensor_reduce(wsum[:], gw[:], AX.X, ALU.add).then_inc(summed, 1)
            dve.tensor_reduce(gate_bs[:], gb[:], AX.X, ALU.add)
            dve.wait_ge(summed, 1)
            for g in range(2):
                dve.tensor_scalar(gate_w[:, :, g, :], mask_hj[:], wsum[:, g:g + 1], None, ALU.mult)
                dve.tensor_scalar(gate_wt[:, :, g, :], mask_h[:], wsum[:, g:g + 1], None, ALU.mult)
            dve.tensor_scalar(far_t[:], far_mask[:, 0, :], far_ends[:, 0:1], None, ALU.mult).then_inc(far_part, 1)
            dve.wait_ge(far_part, 1)
            dve.scalar_tensor_tensor(out=far_c[:], in0=far_mask[:, 1, :], scalar=far_ends[:, 1:2], in1=far_t[:],
                                     op0=ALU.mult, op1=ALU.add)
            dve.wait_ge(line_ready, 2)
            dve.tensor_copy(line[:, 0:512], pl[:, 0, :])
            dve.tensor_copy(line[:, 512:LINE], pl[:, 1, 0:LINE - 512]).then_inc(line_copied, 1)
            dve.wait_ge(slab_loaded, 16 * H)
            dve.tensor_copy(slab[:], falling[:, :, ::-1]).then_inc(slab_ready, 1)
            dve.wait_ge(slab_ready, 1)
            for n, (lo, hi) in enumerate(((0, LO - P), (LO + 2 * P, BAND))):
                dve.tensor_tensor(slab[:, :, lo:hi], slab[:, :, lo:hi],
                                  ends[:, n, :].rearrange("p (h o) -> p h o", o=1).to_broadcast([P, H, hi - lo]),
                                  ALU.subtract).then_inc(slab_ready, 1)


def project(nc, a, q_d, k_d, far_d, v_d, gate_d, gate_w, gate_wt, gate_bs, far_c):
    HT = N // 2
    NU = 4
    NS = NU + 1
    STORES = NS + 1
    with ExitStack() as es:
        def sb(name, shape, dt=F32):
            return es.enter_context(nc.sbuf_tensor(name, shape, dt))

        def sem(name):
            return es.enter_context(nc.semaphore(name))

        w_qk = sb("w_qk", [P, 2, EC, E])
        b_qk = sb("b_qk", [P, 2, EC])
        w_v = sb("w_v", [P, EC, E])
        b_v = sb("b_v", [P, E])
        gc_hj = sb("gc_hj", [P, 1])
        gc_h = sb("gc_h", [P, H])
        xt = sb("xt", [P, 2, EC, HT])
        full = sb("full", [P, NS, HT])
        rest = sb("rest", [P, NS, HT])
        parts = sb("parts", [P, 2, NS, 3, HT], BF16)
        sig = sb("sig", [P, 2, HT])
        gmix = sb("gmix", [P, HT])
        gout = sb("gout", [P, HT])
        vt = sb("vt", [P, 2, 4, H, 2 * D])
        gsig = sb("gsig", [P, 2, 4, H])
        gt1 = sb("gt1", [P, 4, H])
        gt2 = sb("gt2", [P, 4, H])
        gtok = sb("gtok", [P, HQ, NI, 4])
        pu = es.enter_context(nc.psum_tensor("pu", [P, 4, 512], F32))
        pv = es.enter_context(nc.psum_tensor("pv", [P, 2, 2, E], F32))
        pg = es.enter_context(nc.psum_tensor("pg", [P, 4, 2, H], F32))
        loaded, x_loaded = sem("w_loaded"), [sem("x_loaded0"), sem("x_loaded1")]
        unit_done, qk_full, far_full = sem("unit_done"), sem("qk_full"), sem("far_full")
        high_done, rest_done, mid_done, low_done = (sem(x) for x in ("high_done", "rest_done", "mid_done", "low_done"))
        sig_done, mix_step = sem("sig_done"), sem("mix_step")
        v_done, v_read, v_set = sem("v_done"), sem("v_read"), sem("v_set")
        gl_done = [sem("gl_done0"), sem("gl_done1")]
        gl_read, g_step, gtok_done = sem("gl_read"), sem("g_step"), sem("gtok_done")
        stored = [sem("stored0"), sem("stored1")]
        g_stored = sem("g_stored")
        weights = [(w_qk[:, 0], a["wq"].rearrange("(c p) n -> p c n", p=P)), (w_qk[:, 1], a["wk"].rearrange("(c p) n -> p c n", p=P)),
                   (w_v[:], a["wv"].rearrange("(c p) n -> p c n", p=P)), (b_qk[:, 0], a["bq"]), (b_qk[:, 1], a["bk"]),
                   (b_v[:], a["bv"]), (gc_hj[:], a["gc_hj"]), (gc_h[:], a["gc_h"])]
        block = es.enter_context(nc.Block())

        @block.sync
        def _(sp):
            with nc.allow_non_contiguous_dma(reason="small weights, once"):
                for to, of in weights:
                    sp.dma_start(to, of).then_inc(loaded, 16)

            def load(b, s):
                sp.wait_ge(gl_done[s], b)
                sp.dma_start(xt[:, s], a["xt"][bass.ds(b, 1), :, s * HT:(s + 1) * HT].rearrange("o (c p) n -> p (o c) n", p=P)).then_inc(x_loaded[s], 16)

            def store(b, s):
                t0 = s * HT
                sp.wait_ge(low_done, (2 * b + s + 1) * NS)
                for u in range(NU):
                    rows = slice((u % 2) * P, (u % 2 + 1) * P)
                    sp.dma_start((q_d, k_d)[u // 2][:, bass.ds(b, 1), rows, t0:t0 + HT].rearrange("s o p n -> p (s o) n"), parts[:, s, u]).then_inc(stored[s], 16)
                sp.dma_start(far_d[:, bass.ds(b, 1), :, t0:t0 + HT].rearrange("s o p n -> p (s o) n"), parts[:, s, NU]).then_inc(stored[s], 16)
                sp.wait_ge(v_read, (2 * b + s + 1) * 4)
                sp.dma_start(v_d[bass.ds(b * N + t0, HT), :].rearrange("(k p) n -> p k n", p=P),
                             vt[:, s].rearrange("p k h d -> p k (h d)")).then_inc(stored[s], 16)
                if s == 1:
                    sp.wait_ge(gtok_done, 2 * b + 2)
                    sp.dma_start(gate_d[bass.ds(b, 1)].rearrange("o p n -> p (o n)"), gtok[:].rearrange("p a i h -> p (a i h)")).then_inc(g_stored, 16)

            load(0, 0)
            load(0, 1)
            with sp.Fori(0, B - 1) as b:
                for s in range(2):
                    store(b, s)
                    load(b + 1, s)
            store(B - 1, 0)
            store(B - 1, 1)
            for s in range(2):
                sp.wait_ge(stored[s], 16 * STORES * B)
            sp.wait_ge(g_stored, 16 * B)

        @block.gpsimd
        def _(pool):
            pool.memset(vt[:], 0.0).then_inc(v_set, 1)
            with pool.Fori(0, 2 * B, 2) as h0:
                for s in range(2):
                    for u in range(NS):
                        pool.wait_ge(mid_done, (h0 + s) * NS + u + 1)
                        pool.tensor_tensor(parts[:, s, u, 2, :], rest[:, u, :], parts[:, s, u, 1, :], ALU.subtract).then_inc(low_done, 1)

        @block.tensor
        def _(pe):
            pe.wait_ge(loaded, 16 * len(weights))
            with pe.Fori(0, B) as b:
                for s in range(2):
                    h = 2 * b + s
                    pe.wait_ge(x_loaded[s], 16 * (b + 1))
                    for u in range(NU + 2):
                        if u < 2:
                            pe.wait_ge(sig_done, 2 * h)
                        elif u < NU:
                            pe.wait_ge(qk_full, NU * h)
                        else:
                            pe.wait_ge(qk_full, NU * h + u - NU + 1)
                        w = w_qk[:, u // 2, :, (u % 2) * P:(u % 2 + 1) * P] if u < NU else gate_w[:, :, u - NU, :]
                        for c in range(EC):
                            mm = pe.matmul(pu[:, u % 4, :], w[:, c, :], xt[:, s, c, :], start=c == 0, stop=c == EC - 1)
                        mm.then_inc(unit_done, 1)
                    pe.wait_ge(v_read, 4 * h)
                    for t in range(4):
                        for c in range(EC):
                            mm = pe.matmul(pv[:, t // 2, t % 2, :], xt[:, s, c, t * P:(t + 1) * P], w_v[:, c, :], start=c == 0, stop=c == EC - 1)
                        if t % 2 == 1:
                            mm.then_inc(v_done, 1)
                    pe.wait_ge(gl_read, 2 * h)
                    for t in range(4):
                        for c in range(EC):
                            mm = pe.matmul(pg[:, t].rearrange("p g h -> p (g h)"), xt[:, s, c, t * P:(t + 1) * P],
                                           gate_wt[:, c].rearrange("p g h -> p (g h)"), start=c == 0, stop=c == EC - 1)
                    mm.then_inc(gl_done[s], 1)

        @block.scalar
        def _(act):
            act.wait_ge(loaded, 16 * len(weights))
            with act.Fori(0, B) as b:
                for s in range(2):
                    h = 2 * b + s

                    def middle(u):
                        act.wait_ge(rest_done, h * NS + u + 1)
                        act.activation(parts[:, s, u, 1, :], rest[:, u, :], ACT.Copy).then_inc(mid_done, 1)

                    act.wait_ge(stored[s], 16 * STORES * b)
                    for u in range(NU):
                        act.wait_ge(qk_full, h * NU + u + 1)
                        act.activation(parts[:, s, u, 0, :], full[:, u, :], ACT.Copy).then_inc(high_done, 1)
                        if u > 0:
                            middle(u - 1)
                    middle(NU - 1)
                    act.wait_ge(mix_step, 2 * h)
                    for g in range(2):
                        act.wait_ge(unit_done, h * (NU + 2) + NU + g + 1)
                        act.activation(sig[:, g, :], pu[:, g, :], ACT.Sigmoid, bias=gate_bs[:, g:g + 1]).then_inc(sig_done, 1)
                    act.wait_ge(gl_done[s], b + 1)
                    act.wait_ge(g_step, 2 * h)
                    for g in range(2):
                        act.activation(gsig[:, g], pg[:, :, g, :], ACT.Sigmoid, bias=gate_bs[:, g:g + 1]).then_inc(gl_read, 1)
                    act.wait_ge(far_full, h + 1)
                    act.activation(parts[:, s, NU, 0, :], full[:, NU, :], ACT.Copy).then_inc(high_done, 1)
                    middle(NU)

        @block.vector
        def _(dve):
            dve.wait_ge(loaded, 16 * len(weights))
            dve.wait_ge(v_set, 1)
            with dve.Fori(0, B) as b:
                for s in range(2):
                    h = 2 * b + s

                    def rest_of(u):
                        dve.wait_ge(high_done, h * NS + u + 1)
                        dve.tensor_tensor(rest[:, u, :], full[:, u, :], parts[:, s, u, 0, :], ALU.subtract).then_inc(rest_done, 1)

                    dve.wait_ge(low_done, h * NS)
                    for u in range(NU):
                        dve.wait_ge(unit_done, h * (NU + 2) + u + 1)
                        scale = 1.0 / math.sqrt(D) if u < 2 else 1.0
                        dve.tensor_scalar(full[:, u, :], pu[:, u, :], b_qk[:, u // 2, u % 2:u % 2 + 1], scale, ALU.add, ALU.mult).then_inc(qk_full, 1)
                        if u > 0:
                            rest_of(u - 1)
                    rest_of(NU - 1)
                    dve.wait_ge(stored[s], 16 * STORES * b)
                    for t in range(4):
                        dve.wait_ge(v_done, 2 * h + t // 2 + 1)
                        dve.tensor_tensor(vt[:, s, t, :, 0:D], pv[:, t // 2, t % 2, :].rearrange("p (h d) -> p h d", d=D),
                                          b_v[:].rearrange("p (h d) -> p h d", d=D), ALU.add).then_inc(v_read, 1)
                    dve.wait_ge(sig_done, 2 * h + 2)
                    dve.tensor_scalar(gmix[:], sig[:, 1, :], gc_hj[:, 0:1], -1.0, ALU.mult, ALU.add).then_inc(mix_step, 1)
                    dve.wait_ge(mix_step, 2 * h + 1)
                    dve.tensor_tensor(gout[:], sig[:, 0, :], gmix[:], ALU.mult).then_inc(mix_step, 1)
                    dve.wait_ge(mix_step, 2 * h + 2)
                    for i in range(4):
                        ins = dve.tensor_scalar(full[:, NU, i * P:(i + 1) * P], gout[:, i * P:(i + 1) * P], 2.0,
                                                far_c[:, 4 * s + i:4 * s + i + 1], ALU.add, ALU.mult)
                    ins.then_inc(far_full, 1)
                    dve.wait_ge(gl_read, 2 * h + 2)
                    dve.tensor_tensor(gt1[:], gsig[:, 1], gc_h[:].rearrange("p (o h) -> p o h", o=1).to_broadcast([P, 4, H]), ALU.mult).then_inc(g_step, 1)
                    dve.wait_ge(g_step, 2 * h + 1)
                    dve.scalar_tensor_tensor(out=gt2[:], in0=gt1[:], scalar=-1.0, in1=gsig[:, 0], op0=ALU.add, op1=ALU.mult).then_inc(g_step, 1)
                    dve.wait_ge(g_step, 2 * h + 2)
                    if s == 0:
                        dve.wait_ge(g_stored, 16 * b)
                    for i in range(4):
                        ins = dve.tensor_scalar(gtok[:, :, 4 * s + i, :], gt2[:, i, :].rearrange("p (a h) -> p a h", h=4), 2.0, None, ALU.add)
                    ins.then_inc(gtok_done, 1)
                    rest_of(NU)


SIDE = (NI - 1) * P - LO
WIDE = SIDE + N + LO


def window(i):
    return SIDE - (i * P - LO)


def attend(nc, a, q_d, k_d, far_d, v_d, gate_d, slab_d, ot_d, ident):
    R = NI * 4
    with ExitStack() as es:
        def sb(name, shape, dt=F32):
            return es.enter_context(nc.sbuf_tensor(name, shape, dt))

        def sem(name):
            return es.enter_context(nc.semaphore(name))

        qs = [sb(f"qs{k}", [P, 4, N], BF16) for k in range(2)]
        ks = [sb(f"ks{k}", [P, 4, N], BF16) for k in range(2)]
        vs = [sb(f"vs{k}", [P, NI, P]) for k in range(2)]
        gs = [sb(f"gs{k}", [P, NI, 4]) for k in range(2)]
        slab = sb("slab_a", [P, 4, BAND])
        ind = sb("ind", [P, N])
        gbias = [sb(f"gbias{k}", [P, WIDE]) for k in range(4)]
        probs = sb("probs", [P, 2, N])
        pts = sb("pts", [P, 2, 4, NI, P])
        negm = sb("negm", [P, 4])
        sums = sb("sums", [P, 2, 4])
        rsum = sb("rsum", [P, 2, 4])
        rs = sb("rs", [P, 2, 4, 32])
        rsb = sb("rsb", [P, P])
        ot = sb("ot", [P, 2, N])
        sc = es.enter_context(nc.psum_tensor("sc", [P, 2, N], F32))
        pt = es.enter_context(nc.psum_tensor("pt", [P, 3, 4, P], F32))
        pop = es.enter_context(nc.psum_tensor("pop", [P, 2, 256], F32))
        po, pr = pop[:, 0, 0:P], pop[:, 1, 0:P]
        zeros_set, gbias_done, waited, pool_waited = (sem(x) for x in ("zeros_set", "gbias_done", "waited", "pool_waited"))
        ind_in, consts_set = sem("ind_in"), sem("consts_set")
        in_ready = [sem("in_ready0"), sem("in_ready1")]
        slab_in = sem("slab_in")
        scores_done, biased, max_done, exp_done = (sem(x) for x in ("scores_done", "biased", "max_done", "exp_done"))
        tr_done = sem("tr_done")
        copied_a, copied_v = sem("copied_a"), sem("copied_v")
        av_done, recip_done, rs_done, rcopied = (sem(x) for x in ("av_done", "recip_done", "rs_done", "rcopied"))
        ot_done = [sem("ot_done0"), sem("ot_done1")]
        ot_stored = [sem("ot_stored0"), sem("ot_stored1")]
        LOADS = 17
        block = es.enter_context(nc.Block())

        def by_scalar(r, half):
            return half == 0 or r % 4 == 0

        def halves(r, half):
            n = [by_scalar(x // 2, x % 2) for x in range(2 * r + half + 1)]
            return sum(n), len(n) - sum(n)

        def bank(k, r, half):
            return ((k * R + r) * 2 + half) % 3

        SA, SV = halves(R - 1, 1)
        rows = [(k, r) for k in range(2) for r in range(R)]

        def blocks_before(m, k, i):
            return m * NI + (i - 1 if i > 0 or k > 0 else 0)

        @block.sync
        def _(sp):
            sp.dma_start(ind[96:128, :], a["c_ind"]).then_inc(ind_in, 16)
            sp.wait_ge(consts_set, 10)
            with sp.Fori(0, HQ) as g:
                with sp.Fori(0, B // 2) as bb:
                    for k in range(2):
                        b = bb * 2 + k
                        if k == 1:
                            sp.wait_ge(gbias_done, (g * (B // 2) + bb) * (2 * R))
                            sp.dma_start(slab[:], slab_d[:, bass.ds(g * 4, 4), :]).then_inc(slab_in, 16)
                        sp.wait_ge(ot_done[k], (g * (B // 2) + bb) * NI)
                        for s in range(6):
                            sp.dma_start(ks[k][D * s:D * s + D], k_d[PIECES_K[s], bass.ds(b, 1), bass.ds(g * 64, 64), :].rearrange("o (h d) n -> d (o h) n", d=D)).then_inc(in_ready[k], 16)
                            sp.dma_start(qs[k][D * s:D * s + D], q_d[PIECES_Q[s], bass.ds(b, 1), bass.ds(g * 64, 64), :].rearrange("o (h d) n -> d (o h) n", d=D)).then_inc(in_ready[k], 16)
                        for s in range(3):
                            sp.dma_start(qs[k][96 + 8 * s:104 + 8 * s], far_d[s, bass.ds(b, 1), bass.ds(g * 32, 32), :].rearrange("o (h j) n -> j (o h) n", j=NI)).then_inc(in_ready[k], 16)
                        sp.dma_start(vs[k][:], v_d[bass.ds(b * N, N), bass.ds(g * P, P)].rearrange("(j p) n -> p j n", p=P)).then_inc(in_ready[k], 16)
                        sp.dma_start(gs[k][:].rearrange("p i h -> p (i h)"), gate_d[bass.ds(b, 1), :, bass.ds(g * 32, 32)].rearrange("o p n -> p (o n)")).then_inc(in_ready[k], 16)

        @block.gpsimd
        def _(pool):
            for t in gbias:
                pool.memset(t[:], 0.0).then_inc(zeros_set, 1)
            pool.wait_ge(zeros_set, 4)
            with pool.Fori(0, HQ) as g:
                with pool.Fori(0, B // 2) as bb:
                    pair = pool.snap(g * (B // 2) + bb)
                    for k in range(2):
                        pool.wait_ge(in_ready[k], (pair + 1) * (16 * LOADS))
                        if k == 0:
                            pool.wait_ge(slab_in, (pair + 1) * 16)
                        for r in range(R):
                            m = pair * 2 + k
                            pool.wait_ge(max_done, m * R + (r - 3 if k > 0 or r > 3 else 0))
                            pool.sem_inc(pool_waited, 1)
                            pool.tensor_scalar(gbias[r % 4][:, SIDE:SIDE + BAND], slab[:, r % 4, :], gs[k][:, r // 4, r % 4:r % 4 + 1], 1.0,
                                               ALU.mult, ALU.mult).then_inc(gbias_done, 1)

        @block.tensor
        def _(pe):
            pe.wait_ge(consts_set, 10)
            with pe.Fori(0, HQ) as g:
                with pe.Fori(0, B // 2) as bb:
                    pair = pe.snap(g * (B // 2) + bb)

                    def scores(k, r):
                        i, hh = r // 4, r % 4
                        if r == 0:
                            pe.wait_ge(in_ready[k], (pair + 1) * (16 * LOADS))
                        for c in range(2):
                            mm = pe.matmul(sc[:, r % 2, c * 512:(c + 1) * 512], qs[k][:, hh, i * P:(i + 1) * P],
                                           ks[k][:, hh, c * 512:(c + 1) * 512], start=True, stop=True)
                        mm.then_inc(scores_done, 1)

                    def turn(k, r):
                        m = pair * 2 + k
                        for half in range(2):
                            q = (k * R + r) * 2 + half - 3
                            if q >= 0:
                                k0, h0 = q // (2 * R), q % (2 * R)
                                na, nv = halves(h0 // 2, h0 % 2)
                                if by_scalar(h0 // 2, h0 % 2):
                                    pe.wait_ge(copied_a, (pair * 2 + k0) * SA + na)
                                else:
                                    pe.wait_ge(copied_v, (pair * 2 + k0) * SV + nv)
                            for j in range(4):
                                jj = 4 * half + j
                                mm = pe.transpose(pt[:, bank(k, r, half), j, :], probs[:, r % 2, jj * P:(jj + 1) * P], ident[:])
                            mm.then_inc(tr_done, 1)

                    def weigh(k, i, part):
                        m = pair * 2 + k
                        if part == 0:
                            na, nv = halves(4 * i + 3, 1)
                            pe.wait_ge(copied_a, m * SA + na)
                            pe.wait_ge(copied_v, m * SV + nv)
                            if i > 0:
                                pe.wait_ge(ot_done[k], pair * NI + i)
                            elif k == 1:
                                pe.wait_ge(ot_done[0], (pair + 1) * NI)
                            else:
                                pe.wait_ge(ot_done[1], pair * NI)
                        for j in range(2 * part, 2 * part + 2):
                            for hh in range(4):
                                mm = pe.matmul(po[32 * hh:32 * hh + 32], vs[k][:, j, 32 * hh:32 * hh + 32], pts[:, i % 2, hh, j, :],
                                               start=j == 0, stop=j == NI - 1, skip_group_check=True)
                        if part == 3:
                            pe.wait_ge(rs_done, m * NI + i + 1)
                            pe.transpose(pr, rs[:, i % 2, :, :].rearrange("p h o -> p (h o)"), ident[:]).then_inc(av_done, 1)

                    scores(*rows[0])
                    scores(*rows[1])
                    for x in range(len(rows) + 4):
                        if x < len(rows):
                            pe.wait_ge(exp_done, (pair * 2 + rows[x][0]) * R + rows[x][1] + 1)
                            if x + 2 < len(rows):
                                scores(*rows[x + 2])
                            turn(*rows[x])
                        if x >= 4:
                            k, r = rows[x - 4]
                            weigh(k, r // 4, r % 4)

        @block.vector
        def _(dve):
            for k in range(2):
                dve.memset(qs[k][96:128], 0.0).then_inc(consts_set, 1)
            dve.wait_ge(ind_in, 16)
            for k in range(2):
                for hh in range(4):
                    dve.tensor_copy(ks[k][96:128, hh, :], ind[96:128, :]).then_inc(consts_set, 1)
            with dve.Fori(0, HQ) as g:
                with dve.Fori(0, B // 2) as bb:
                    pair = dve.snap(g * (B // 2) + bb)

                    def bias_and_max(k, r):
                        m = pair * 2 + k
                        dve.wait_ge(gbias_done, m * R + r + 1)
                        dve.wait_ge(scores_done, m * R + r + 1)
                        dve.sem_inc(waited, 1)
                        w = window(r // 4)
                        dve.tensor_tensor_reduce(sc[:, r % 2, :], sc[:, r % 2, :], gbias[r % 4][:, w:w + N], -1.0, 3.0e38,
                                                 ALU.add, ALU.min, negm[:, r % 4:r % 4 + 1]).then_inc(max_done, 1)

                    def copy_out(k, r):
                        m = pair * 2 + k
                        i, hh = r // 4, r % 4
                        if not by_scalar(r, 1):
                            dve.wait_ge(tr_done, (m * R + r + 1) * 2)
                            if hh == 1:
                                dve.wait_ge(av_done, blocks_before(m, k, i))
                            dve.tensor_copy(pts[:, i % 2, hh, 4:8, :], pt[:, bank(k, r, 1)]).then_inc(copied_v, 1)

                    def reciprocals(k, i):
                        m = pair * 2 + k
                        dve.wait_ge(exp_done, m * R + 4 * i + 4)
                        dve.reciprocal(rsum[:, i % 2, :], sums[:, i % 2, :]).then_inc(recip_done, 1)
                        dve.wait_ge(recip_done, m * NI + i + 1)
                        dve.wait_ge(av_done, blocks_before(m, k, i))
                        dve.tensor_copy(rs[:, i % 2], rsum[:, i % 2, :].rearrange("p (h o) -> p h o", o=1).to_broadcast([P, 4, 32])).then_inc(rs_done, 1)

                    def finish(k, i):
                        m = pair * 2 + k
                        if i == 0:
                            dve.wait_ge(ot_stored[k], pair * 16)
                        dve.wait_ge(rcopied, m * NI + i + 1)
                        dve.wait_ge(av_done, m * NI + i + 1)
                        dve.tensor_tensor(ot[:, k, i * P:(i + 1) * P], po, rsb[:], ALU.mult).then_inc(ot_done[k], 1)

                    for x in range(len(rows) + 5):
                        if x < len(rows):
                            bias_and_max(*rows[x])
                        if 1 <= x <= len(rows):
                            k, r = rows[x - 1]
                            copy_out(k, r)
                            if r % 4 == 3:
                                reciprocals(k, r // 4)
                        if x >= 5 and rows[x - 5][1] % 4 == 3:
                            finish(rows[x - 5][0], rows[x - 5][1] // 4)

        @block.scalar
        def _(act):
            with act.Fori(0, HQ) as g:
                with act.Fori(0, B // 2) as bb:
                    pair = act.snap(g * (B // 2) + bb)

                    def exponential(k, r):
                        m = pair * 2 + k
                        i, hh = r // 4, r % 4
                        act.wait_ge(max_done, m * R + r + 1)
                        if k > 0 or r >= 2:
                            act.wait_ge(tr_done, (m * R + r - 1) * 2)
                        if hh == 0:
                            act.wait_ge(rs_done, blocks_before(m, k, i))
                        act.activation(probs[:, r % 2, :], sc[:, r % 2, :], ACT.Exp, bias=negm[:, r % 4:r % 4 + 1], scale=-1.0,
                                       accum_out=sums[:, i % 2, hh:hh + 1]).then_inc(exp_done, 1)

                    def copy_out(k, r):
                        m = pair * 2 + k
                        i, hh = r // 4, r % 4
                        for half in range(2):
                            if by_scalar(r, half):
                                act.wait_ge(tr_done, (m * R + r) * 2 + half + 1)
                                if hh == 0 and half == 0:
                                    act.wait_ge(av_done, blocks_before(m, k, i))
                                act.activation(pts[:, i % 2, hh, 4 * half:4 * half + 4, :], pt[:, bank(k, r, half)], ACT.Copy).then_inc(copied_a, 1)

                    def copy_sums(k, i):
                        m = pair * 2 + k
                        act.wait_ge(av_done, m * NI + i + 1)
                        act.activation(rsb[:], pr, ACT.Copy).then_inc(rcopied, 1)

                    def store(k):
                        act.wait_ge(ot_done[k], (pair + 1) * NI)
                        act.dma_start(ot_d[bass.ds(g, 1), bass.ds(bb * 2 + k, 1)].rearrange("o w p n -> p (o w n)"), ot[:, k, :]).then_inc(ot_stored[k], 16)

                    for x in range(len(rows) + 5):
                        if x == R + 10:
                            store(0)
                        if x < len(rows):
                            exponential(*rows[x])
                        if 1 <= x <= len(rows):
                            copy_out(*rows[x - 1])
                        if x >= 5 and rows[x - 5][1] % 4 == 3:
                            copy_sums(rows[x - 5][0], rows[x - 5][1] // 4)
                    store(1)
            for k in range(2):
                act.wait_ge(ot_stored[k], 16 * HQ * B // 2)


def merge(nc, a, ot_d, xg_d, ident, logits):
    with ExitStack() as es:
        def sb(name, shape, dt=F32):
            return es.enter_context(nc.sbuf_tensor(name, shape, dt))

        def sem(name):
            return es.enter_context(nc.semaphore(name))

        TC = 2
        NCH = NI // TC
        w_o = sb("w_o", [P, HQ, E])
        b_o = sb("b_o", [P, E])
        w_r = sb("w_r", [P, EC, NE])
        otl = sb("otl", [P, 2, HQ, TC * P])
        xr = sb("xr", [P, 2, TC, E])
        xb = sb("xb", [P, 2, TC, E])
        y = sb("y", [P, 2, E])
        stats = sb("stats", [P, TC, 6])
        mv = sb("mv", [P, TC, 2])
        std = sb("std", [P, TC])
        rstd = sb("rstd", [P, TC])
        eps = sb("eps", [P, 1])
        x1 = sb("x1", [P, 2, E])
        x1t = sb("x1t", [P, 2, E])
        py = es.enter_context(nc.psum_tensor("py", [P, 2, 512], F32))
        px = es.enter_context(nc.psum_tensor("px", [P, 2, 512], F32))
        pl = es.enter_context(nc.psum_tensor("plg", [P, 2, 512], F32))
        loaded, w_zero = sem("mw_loaded"), sem("w_zero")
        in_ready = [sem("m_in0"), sem("m_in1")]
        y_done, x_biased, added, stat_done, mean_done, std_done, rstd_done, x1_done = (
            sem("m_" + n) for n in ("y_done", "x_biased", "added", "stat_done", "mean_done", "std_done", "rstd_done", "x1_done"))
        turned, turned_out, routed, logits_out = (sem("m_" + n) for n in ("turned", "turned_out", "routed", "logits_out"))
        x1_stored = [sem("x1_stored0"), sem("x1_stored1")]
        stat_seen = sem("m_stat_seen")
        tiles = [(c, t) for c in range(NCH) for t in range(TC)]
        block = es.enter_context(nc.Block())

        @block.sync
        def _(sp):
            with nc.allow_non_contiguous_dma(reason="small weights, once"):
                sp.dma_start(b_o[:], a["bo"]).then_inc(loaded, 16)
                sp.dma_start(w_r[:], a["wr"].rearrange("(c p) n -> p c n", p=P)).then_inc(loaded, 16)
            sp.wait_ge(w_zero, 1)
            for h in range(4):
                sp.dma_start(w_o[32 * h:32 * h + D], a["wo"].rearrange("(g h d) n -> h d g n", h=4, d=D)[h]).then_inc(loaded, 16)
            with sp.Fori(0, B) as b:
                for c in range(NCH):
                    sp.wait_ge(added, b * NI + (c - 1) * TC if c > 0 else b * NI)
                    sp.dma_start(otl[:, c % 2], ot_d[:, bass.ds(b, 1), :, c * TC * P:(c + 1) * TC * P].rearrange("g o p n -> p (g o) n")).then_inc(in_ready[c % 2], 16)
                    sp.dma_start(xr[:, c % 2], a["x"][bass.ds(b * N + c * TC * P, TC * P), :].rearrange("(t p) n -> p t n", p=P)).then_inc(in_ready[c % 2], 16)

        @block.gpsimd
        def _(pool):
            pool.memset(w_o[:], 0.0).then_inc(w_zero, 1)
            pool.memset(eps[:], EPS).then_inc(w_zero, 1)
            pool.wait_ge(loaded, 16 * 6)
            with pool.Fori(0, B) as b:
                for c in range(NCH):
                    q = b * (NCH // 2) + c // 2
                    pool.wait_ge(in_ready[c % 2], (q + 1) * 32)
                    pool.wait_ge(added, b * NI + (c - 1) * TC if c > 0 else b * NI)
                    for t in range(TC):
                        pool.tensor_tensor(xb[:, c % 2, t], xr[:, c % 2, t], b_o[:], ALU.add).then_inc(x_biased, 1)
                    for t in range(TC):
                        n = c * TC + t
                        pool.wait_ge(x1_done, b * NI + n + 1)
                        pool.dma_start(xg_d[bass.ds(b * N + SLOTS + n * P, P), :], x1[:, n % 2]).then_inc(x1_stored[n % 2], 16)
            for k in range(2):
                pool.wait_ge(x1_stored[k], 16 * TT // 2)

        @block.tensor
        def _(pe):
            pe.wait_ge(loaded, 16 * 6)
            with pe.Fori(0, B) as b:
                def project_out(c, t):
                    n = c * TC + t
                    if t == 0:
                        pe.wait_ge(in_ready[c % 2], (b * (NCH // 2) + c // 2 + 1) * 32)
                    if n >= 2:
                        pe.wait_ge(added, b * NI + n - 1)
                    for g in range(HQ):
                        mm = pe.matmul(py[:, n % 2, 0:E], otl[:, c % 2, g, t * P:(t + 1) * P], w_o[:, g, :], start=g == 0, stop=g == HQ - 1)
                    mm.then_inc(y_done, 1)

                def turn_and_route(n):
                    pe.wait_ge(x1_done, b * NI + n + 1)
                    if n >= 2:
                        pe.wait_ge(turned_out, b * NI + n - 1)
                    for k in range(EC):
                        mm = pe.transpose(px[:, n % 2, k * P:(k + 1) * P], x1[:, n % 2, k * P:(k + 1) * P], ident[:])
                    mm.then_inc(turned, 1)
                    pe.wait_ge(turned_out, b * NI + n + 1)
                    pe.wait_ge(logits_out, b * NI + max(n - 1, 0))
                    for k in range(EC):
                        mm = pe.matmul(pl[:, n % 2, 0:NE], x1t[:, n % 2, k * P:(k + 1) * P], w_r[:, k, :], start=k == 0, stop=k == EC - 1)
                    mm.then_inc(routed, 1)

                project_out(*tiles[0])
                project_out(*tiles[1])
                for n in range(NI):
                    if n % TC == 0:
                        for t in range(TC):
                            if n + TC + t < NI:
                                project_out(*tiles[n + TC + t])
                    turn_and_route(n)

        @block.scalar
        def _(act):
            act.wait_ge(w_zero, 2)
            with act.Fori(0, B) as b:
                for c in range(NCH):
                    act.wait_ge(mean_done, b * NI + (c + 1) * TC)
                    act.activation(std[:], mv[:, :, 1], ACT.Sqrt, bias=eps[:, 0:1]).then_inc(std_done, 1)
                    for t in range(TC):
                        n = c * TC + t
                        act.wait_ge(turned, b * NI + n + 1)
                        act.activation(x1t[:, n % 2], px[:, n % 2, 0:E], ACT.Copy).then_inc(turned_out, 1)

        @block.vector
        def _(dve):
            with dve.Fori(0, B) as b:
                def logits_out_of(c):
                    for t in range(TC):
                        n = c * TC + t
                        dve.wait_ge(routed, b * NI + n + 1)
                        dve.tensor_copy(logits[:, bass.ds(b * NI + n, 1), :], pl[:, t:t + 1, 0:NE]).then_inc(logits_out, 1)

                for c in range(NCH):
                    n0 = b * NI + c * TC
                    for t in range(TC):
                        dve.wait_ge(y_done, n0 + t + 1)
                        dve.wait_ge(x_biased, n0 + t + 1)
                        dve.tensor_tensor(y[:, t], py[:, t, 0:E], xb[:, c % 2, t], ALU.add).then_inc(added, 1)
                    for t in range(TC):
                        dve.wait_ge(added, n0 + t + 1)
                        dve.bn_stats(stats[:, t], y[:, t]).then_inc(stat_done, 1)
                    dve.wait_ge(stat_done, n0 + TC)
                    dve.sem_inc(stat_seen, 1)
                    for t in range(TC):
                        dve.bn_aggr(mv[:, t], stats[:, t]).then_inc(mean_done, 1)
                    if c > 0:
                        logits_out_of(c - 1)
                    dve.wait_ge(std_done, b * NCH + c + 1)
                    dve.reciprocal(rstd[:], std[:]).then_inc(rstd_done, 1)
                    dve.wait_ge(rstd_done, b * NCH + c + 1)
                    for t in range(TC):
                        dve.wait_ge(x1_stored[t], (b * NCH + c) * 16)
                        if c > 0:
                            dve.wait_ge(turned, b * NI + (c - 1) * TC + t + 1)
                        dve.tensor_scalar(x1[:, t], y[:, t], mv[:, t, 0:1], rstd[:, t:t + 1], ALU.subtract, ALU.mult).then_inc(x1_done, 1)
                logits_out_of(NCH - 1)


def route(nc, a, xg_d, zeroed, logits, slot_s, slot_g, wgt):
    with ExitStack() as es:
        def sb(name, shape, dt=F32):
            return es.enter_context(nc.sbuf_tensor(name, shape, dt))

        def sem(name):
            return es.enter_context(nc.semaphore(name))

        wide = [P, TT, NE]
        lz, pr, oh1, oh2, tmp, taken = (sb("r_" + n, wide) for n in ("lz", "pr", "oh1", "oh2", "tmp", "taken"))
        m1, m2, s1, s2, best, nfb, elig, incl, pos, kept, over, ones, fbm = (
            sb("r_" + n, [P, TT]) for n in ("m1", "m2", "s1", "s2", "best", "nfb", "elig", "incl", "pos", "kept", "over", "ones", "fbm"))
        order = sb("r_order", [P, NE])
        token = sb("r_token", [P, TT])
        before = sb("r_before", [P, P])
        all1 = sb("r_all1", [P, P])
        xs = sb("r_xs", [P, 2, E])
        idx = sb("r_idx", [P, 2, TOPK], U32)
        pp = es.enter_context(nc.psum_tensor("r_pp", [P, 2, 512], F32))
        loaded, step, shifted, exped, elig_done, counted, slots_done = (
            sem("r_" + n) for n in ("loaded", "step", "shifted", "exped", "elig_done", "counted", "slots_done"))
        xs_in = [sem("r_xs0"), sem("r_xs1")]
        idx_set, idx_seen = sem("r_idx_set"), sem("r_idx_seen")
        scattered = [sem("r_sc0"), sem("r_sc1")]
        block = es.enter_context(nc.Block())

        def over_experts(x):
            return x.rearrange("p (t o) -> p t o", o=1).to_broadcast(wide)

        def over_tiles(x):
            return x.rearrange("p (o e) -> p o e", o=1).to_broadcast(wide)

        @block.sync
        def _(sp):
            sp.dma_start(order[:], a["c_order"]).then_inc(loaded, 16)
            sp.dma_start(token[:], a["c_token"]).then_inc(loaded, 16)
            sp.dma_start(before[:], a["c_before"]).then_inc(loaded, 16)
            with sp.Fori(0, TT // 2) as m:
                for k in range(2):
                    sp.wait_ge(scattered[k], m * 32)
                    sp.dma_start(xs[:, k], xg_d[bass.ds(m * (2 * P) + SLOTS + k * P, P), :]).then_inc(xs_in[k], 16)

        @block.scalar
        def _(act):
            act.wait_ge(shifted, 1)
            act.activation(lz[:], lz[:], ACT.Exp).then_inc(exped, 1)

        @block.tensor
        def _(pe):
            pe.wait_ge(loaded, 48)
            for e in range(NE):
                pe.wait_ge(elig_done, e + 2)
                pe.matmul(pp[:, 0, 0:TT], before[:], elig[:], start=True, stop=True)
                pe.matmul(pp[:, 1, 0:TT], all1[:], elig[:], start=True, stop=True).then_inc(counted, 1)

        @block.vector
        def _(dve):
            chain = [0]

            def then(ins):
                chain[0] += 1
                ins.then_inc(step, 1)
                dve.wait_ge(step, chain[0])

            dve.wait_ge(loaded, 48)
            dve.memset(all1[:], 1.0)
            dve.memset(ones[:], 1.0)
            dve.memset(nfb[:], 1.0).then_inc(elig_done, 1)
            then(dve.tensor_reduce(m1[:], logits[:], AX.X, ALU.max))
            dve.tensor_tensor(lz[:], logits[:], over_experts(m1[:]), ALU.subtract).then_inc(shifted, 1)
            dve.wait_ge(exped, 1)
            then(dve.tensor_reduce(s1[:], lz[:], AX.X, ALU.add))
            then(dve.reciprocal(s2[:], s1[:]))
            then(dve.tensor_tensor(pr[:], lz[:], over_experts(s2[:]), ALU.mult))
            for m, oh in ((m1, oh1), (m2, oh2)):
                then(dve.tensor_reduce(m[:], pr[:], AX.X, ALU.max))
                then(dve.tensor_tensor(tmp[:], pr[:], over_experts(m[:]), ALU.is_equal))
                then(dve.tensor_tensor(tmp[:], tmp[:], over_tiles(order[:]), ALU.mult))
                then(dve.tensor_reduce(best[:], tmp[:], AX.X, ALU.min))
                then(dve.tensor_tensor(oh[:], over_tiles(order[:]), over_experts(best[:]), ALU.is_equal))
                if oh is oh1:
                    then(dve.scalar_tensor_tensor(out=pr[:], in0=oh[:], scalar=-4.0, in1=pr[:], op0=ALU.mult, op1=ALU.add))
            then(dve.tensor_tensor(s1[:], m1[:], m2[:], ALU.add))
            then(dve.tensor_scalar(s1[:], s1[:], 1e-9, None, ALU.max))
            then(dve.reciprocal(s2[:], s1[:]))
            dve.tensor_tensor(m1[:], m1[:], s2[:], ALU.mult)
            then(dve.tensor_tensor(m2[:], m2[:], s2[:], ALU.mult))
            then(dve.tensor_tensor(tmp[:], oh1[:], oh2[:], ALU.add))
            for e in range(NE):
                ins = dve.tensor_tensor(elig[:], tmp[:, :, e], nfb[:], ALU.mult)
                ins.then_inc(elig_done, 1)
                dve.wait_ge(counted, e + 1)
                then(dve.tensor_tensor_scan(incl[:], ones[:], pp[:, 1, 0:TT], 0.0, ALU.mult, ALU.add))
                then(dve.tensor_tensor(pos[:], incl[:], pp[:, 1, 0:TT], ALU.subtract))
                then(dve.tensor_tensor(pos[:], pos[:], pp[:, 0, 0:TT], ALU.add))
                then(dve.scalar_tensor_tensor(out=kept[:], in0=pos[:], scalar=float(CAP), in1=elig[:], op0=ALU.is_lt, op1=ALU.mult))
                dve.scalar_tensor_tensor(out=taken[:, :, e], in0=pos[:], scalar=float(e * CAP), in1=kept[:], op0=ALU.add, op1=ALU.mult)
                then(dve.tensor_tensor(over[:], elig[:], kept[:], ALU.subtract))
                then(dve.tensor_tensor(nfb[:], nfb[:], over[:], ALU.subtract))
            then(dve.tensor_scalar(fbm[:], nfb[:], -1.0, 1.0, ALU.mult, ALU.add))
            then(dve.tensor_tensor(token[:], token[:], fbm[:], ALU.mult))
            for k, (m, oh) in enumerate(((m1, oh1), (m2, oh2))):
                then(dve.tensor_tensor(tmp[:], oh[:], taken[:], ALU.mult))
                then(dve.tensor_reduce(best[:], tmp[:], AX.X, ALU.add))
                then(dve.tensor_tensor(best[:], best[:], nfb[:], ALU.mult))
                dve.tensor_tensor(slot_g[:, :, k], best[:], token[:], ALU.add)
                dve.scalar_tensor_tensor(out=slot_s[:, :, k], in0=fbm[:], scalar=float(ROWS), in1=best[:], op0=ALU.mult, op1=ALU.add)
                then(dve.tensor_tensor(wgt[:, :, k], m[:], nfb[:], ALU.mult))
            dve.tensor_tensor(wgt[:, :, 0], wgt[:, :, 0], fbm[:], ALU.add).then_inc(slots_done, 1)

        @block.gpsimd
        def _(pool):
            last_row = pool.to_reg(ROWS - 1)
            pool.wait_ge(slots_done, 1)
            pool.wait_ge(zeroed, 16 * NZ)
            with pool.Fori(0, TT // 2) as m:
                for k in range(2):
                    t = m * 2 + k
                    pool.wait_ge(scattered[k], m * 32)
                    pool.sem_inc(idx_seen, 1)
                    pool.tensor_copy(idx[:, k:k + 1], slot_s[:, bass.ds(t, 1), :]).then_inc(idx_set, 1)
                    pool.wait_ge(xs_in[k], (m + 1) * 16)
                    pool.wait_ge(idx_set, t + 1)
                    pool.sem_inc(idx_seen, 1)
                    for c in range(TOPK):
                        pool.indirect_dma_start(xg_d, bass.IndirectOffsetOnAxis(idx[:, k, c:c + 1], 0), xs[:, k], None,
                                                bounds_check=last_row, oob_is_err=False).then_inc(scattered[k], 16)
            for k in range(2):
                pool.wait_ge(scattered[k], 32 * (TT // 2))


def ffn(nc, a, xg_d, yg_d, ident):
    networks(nc, a, xg_d, yg_d, ident, "f", SLOTS, T // RT // 2, 2, [NE], False)
    networks(nc, a, xg_d, yg_d, ident, "e", 0, NE // 2, 2 * CAP // RT, [0, 1], True)


def networks(nc, a, xg_d, yg_d, ident, tag, row0, loops, body, nets, moving):
    with ExitStack() as es:
        def sb(name, shape, dt=F32):
            return es.enter_context(nc.sbuf_tensor(tag + name, shape, dt))

        def sem(name):
            return es.enter_context(nc.semaphore(tag + name))

        NW = len(nets)
        per = body // NW
        KB = RT // P
        w1 = sb("w1", [P, NW, EC, HID])
        w2 = sb("w2", [P, NW, HC, E])
        b1 = sb("b1", [P, NW, HC])
        b2 = sb("b2", [P, NW, E])
        xin = sb("xin", [P, 2, KB, E])
        xt = sb("xt", [P, 2, EC, RT])
        hid = sb("hid", [P, 2, HC, RT])
        yo = sb("yo", [P, 2, KB, E])
        px = es.enter_context(nc.psum_tensor(tag + "px", [P, EC, 512], F32))
        ph = es.enter_context(nc.psum_tensor(tag + "ph", [P, 3, 512], F32))
        py = es.enter_context(nc.psum_tensor(tag + "py", [P, 3, 512], F32))
        w_in = [sem(f"w_in{k}") for k in range(NW)]
        x_in = [sem("x_in0"), sem("x_in1")]
        turned, out0, out1, up_done, act_done, down_done, y_out = (
            sem(n) for n in ("turned", "out0", "out1", "up_done", "act_done", "down_done", "y_out"))
        y_stored = [sem("y_stored0"), sem("y_stored1")]
        block = es.enter_context(nc.Block())

        def h_bank(y, h):
            return (y * HC + h) % 3

        def y_bank(y, k):
            return (y * KB + k) % 3

        def rows(t, m, y):
            return t[bass.ds(m * (body * RT) + row0 + y * RT, RT), :].rearrange("(k p) e -> p k e", p=P)

        @block.sync
        def _(sp):
            def load_weights(m, k):
                net = m * 2 + nets[k] if moving else nets[k]
                sp.dma_start(w1[:, k], a["w1"][bass.ds(net, 1)].rearrange("o (c p) n -> p (o c) n", p=P)).then_inc(w_in[k], 16)
                sp.dma_start(w2[:, k], a["w2"][bass.ds(net, 1)].rearrange("o (c p) n -> p (o c) n", p=P)).then_inc(w_in[k], 16)
                sp.dma_start(b1[:, k], a["b1"][bass.ds(net, 1)].rearrange("o p n -> p (o n)")).then_inc(w_in[k], 16)
                sp.dma_start(b2[:, k], a["b2"][bass.ds(net, 1), :].to_broadcast([P, E])).then_inc(w_in[k], 16)

            if not moving:
                load_weights(0, 0)
            with sp.Fori(0, loops) as m:
                for y in range(body):
                    if moving and y % per == 0:
                        sp.wait_ge(y_out, m * (body * KB))
                        load_weights(m, y // per)
                    if y >= 2:
                        sp.wait_ge(turned, m * body + y - 1)
                    else:
                        sp.wait_ge(turned, m * body)
                    sp.dma_start(xin[:, y % 2], rows(xg_d, m, y)).then_inc(x_in[y % 2], 16)

        @block.gpsimd
        def _(pool):
            with pool.Fori(0, loops) as m:
                for y in range(body):
                    pool.wait_ge(y_out, (m * body + y + 1) * KB)
                    pool.dma_start(rows(yg_d, m, y), yo[:, y % 2]).then_inc(y_stored[y % 2], 16)
            for k in range(2):
                pool.wait_ge(y_stored[k], 16 * loops * body // 2)

        @block.tensor
        def _(pe):
            with pe.Fori(0, loops) as m:
                def turn(y):
                    n = m * body + y
                    pe.wait_ge(x_in[y % 2], (m * (body // 2) + y // 2 + 1) * 16)
                    pe.wait_ge(out0, n)
                    pe.wait_ge(out1, n)
                    for c in range(EC):
                        for k in range(KB):
                            mm = pe.transpose(px[:, c, k * P:(k + 1) * P], xin[:, y % 2, k, c * P:(c + 1) * P], ident[:])
                    mm.then_inc(turned, 1)

                def up(y):
                    n, w = m * body + y, y // per
                    if y % per == 0:
                        pe.wait_ge(w_in[w], (m + 1) * 64 if moving else 64)
                    pe.wait_ge(out0, n + 1)
                    pe.wait_ge(out1, n + 1)
                    for h in range(HC):
                        if y > 0 or h >= 3:
                            pe.wait_ge(act_done, n * HC + h - 2)
                        for c in range(EC):
                            mm = pe.matmul(ph[:, h_bank(y, h), :], w1[:, w, c, h * P:(h + 1) * P], xt[:, y % 2, c, :], start=c == 0, stop=c == EC - 1)
                        mm.then_inc(up_done, 1)

                def down(y):
                    n, w = m * body + y, y // per
                    pe.wait_ge(act_done, (n + 1) * HC)
                    for k in range(KB):
                        if y > 0 or k >= 3:
                            pe.wait_ge(y_out, n * KB + k - 2)
                        for h in range(HC):
                            mm = pe.matmul(py[:, y_bank(y, k), 0:E], hid[:, y % 2, h, k * P:(k + 1) * P], w2[:, w, h, :], start=h == 0, stop=h == HC - 1)
                        mm.then_inc(down_done, 1)

                turn(0)
                pe.wait_ge(act_done, m * (body * HC))
                pe.wait_ge(y_out, m * (body * KB))
                for y in range(body):
                    up(y)
                    if y + 1 < body:
                        turn(y + 1)
                    down(y)

        @block.scalar
        def _(act):
            with act.Fori(0, loops) as m:
                def out_of_px(y):
                    n = m * body + y
                    act.wait_ge(turned, n + 1)
                    act.wait_ge(up_done, (n - 1) * HC if y >= 1 else n * HC)
                    act.activation(xt[:, y % 2, 1], px[:, 1, :], ACT.Copy).then_inc(out1, 1)

                out_of_px(0)
                for y in range(body):
                    n, w = m * body + y, y // per
                    act.wait_ge(down_done, (n - 1) * KB if y >= 1 else n * KB)
                    for h in range(HC):
                        act.wait_ge(up_done, n * HC + h + 1)
                        act.activation(hid[:, y % 2, h, :], ph[:, h_bank(y, h), :], ACT.Gelu, bias=b1[:, w, h:h + 1]).then_inc(act_done, 1)
                    if y + 1 < body:
                        out_of_px(y + 1)

        @block.vector
        def _(dve):
            with dve.Fori(0, loops) as m:
                def out_of_px(y):
                    n = m * body + y
                    dve.wait_ge(turned, n + 1)
                    dve.wait_ge(up_done, (n - 1) * HC if y >= 1 else n * HC)
                    dve.tensor_copy(xt[:, y % 2, 0], px[:, 0, :]).then_inc(out0, 1)

                out_of_px(0)
                for y in range(body):
                    n, w = m * body + y, y // per
                    if y + 1 < body:
                        out_of_px(y + 1)
                    dve.wait_ge(y_stored[y % 2], (m * (body // 2) + y // 2) * 16)
                    if y % per == 0:
                        dve.wait_ge(w_in[w], (m + 1) * 64 if moving else 64)
                    for k in range(KB):
                        dve.wait_ge(down_done, n * KB + k + 1)
                        dve.tensor_tensor(yo[:, y % 2, k], py[:, y_bank(y, k), 0:E], b2[:, w], ALU.add).then_inc(y_out, 1)


def combine(nc, a, xg_d, yg_d, slot_g, wgt, out):
    with ExitStack() as es:
        def sb(name, shape, dt=F32):
            return es.enter_context(nc.sbuf_tensor(name, shape, dt))

        def sem(name):
            return es.enter_context(nc.semaphore(name))

        NBUF = 4
        idx = sb("c_idx", [P, NBUF, TOPK], U32)
        w = sb("c_w", [P, NBUF, TOPK])
        yk = [sb(f"c_y{c}", [P, NBUF, E]) for c in range(TOPK)]
        x1 = sb("c_x1", [P, NBUF, E])
        acc = sb("c_acc", [P, NBUF, E])
        tot = sb("c_tot", [P, NBUF, E])
        stats = sb("c_stats", [P, NBUF, 6])
        mv = sb("c_mv", [P, NBUF, 2])
        std = sb("c_std", [P, NBUF])
        rstd = sb("c_rstd", [P, NBUF])
        eps = sb("c_eps", [P, 1])
        res = sb("c_res", [P, NBUF, E])
        idx_seen, stat_seen = sem("c_idx_seen"), sem("c_stat_seen")
        idx_set, w_set, eps_set = sem("c_idx_set"), sem("c_w_set"), sem("c_eps_set")
        gathered = [sem(f"c_g{k}") for k in range(NBUF)]
        x_in = [sem(f"c_x{k}") for k in range(NBUF)]
        stored = [sem(f"c_st{k}") for k in range(NBUF)]
        first, added, stat_done, mean_done, std_done, rstd_done, res_done = (
            sem("c_" + n) for n in ("first", "added", "stat_done", "mean_done", "std_done", "rstd_done", "res_done"))
        block = es.enter_context(nc.Block())

        @block.gpsimd
        def _(pool):
            pool.memset(eps[:], EPS).then_inc(eps_set, 1)
            last_row = pool.to_reg(ROWS - 1)
            with pool.Fori(0, TT // NBUF) as m:
                pool.wait_ge(added, m * NBUF)
                pool.sem_inc(idx_seen, 1)
                pool.tensor_copy(idx[:], slot_g[:, bass.ds(m * NBUF, NBUF), :]).then_inc(idx_set, 1)
                pool.wait_ge(idx_set, m + 1)
                pool.sem_inc(idx_seen, 1)
                for k in range(NBUF):
                    for c in range(TOPK):
                        pool.indirect_dma_start(yk[c][:, k], None, yg_d, bass.IndirectOffsetOnAxis(idx[:, k, c:c + 1], 0),
                                                bounds_check=last_row, oob_is_err=False).then_inc(gathered[k], 16)

        @block.sync
        def _(sp):
            with sp.Fori(0, TT // NBUF) as m:
                for k in range(NBUF):
                    sp.wait_ge(added, m * NBUF)
                    sp.dma_start(x1[:, k], xg_d[bass.ds(m * (NBUF * P) + SLOTS + k * P, P), :]).then_inc(x_in[k], 16)
                for k in range(NBUF):
                    sp.wait_ge(res_done, m * NBUF + k + 1)
                    sp.dma_start(out[bass.ds(m * (NBUF * P) + k * P, P), :], res[:, k]).then_inc(stored[k], 16)
            for k in range(NBUF):
                sp.wait_ge(stored[k], 16 * (TT // NBUF))

        @block.scalar
        def _(act):
            act.wait_ge(eps_set, 1)
            with act.Fori(0, TT // NBUF) as m:
                act.wait_ge(mean_done, (m + 1) * NBUF)
                act.activation(std[:], mv[:, :, 1], ACT.Sqrt, bias=eps[:, 0:1]).then_inc(std_done, 1)

        @block.vector
        def _(dve):
            with dve.Fori(0, TT // NBUF) as m:
                dve.tensor_copy(w[:], wgt[:, bass.ds(m * NBUF, NBUF), :]).then_inc(w_set, 1)
                dve.wait_ge(w_set, m + 1)
                for k in range(NBUF):
                    dve.wait_ge(gathered[k], (m + 1) * 32)
                    dve.wait_ge(x_in[k], (m + 1) * 16)
                    dve.scalar_tensor_tensor(out=acc[:, k], in0=yk[0][:, k], scalar=w[:, k, 0:1], in1=x1[:, k], op0=ALU.mult, op1=ALU.add).then_inc(first, 1)
                for k in range(NBUF):
                    dve.wait_ge(first, m * NBUF + k + 1)
                    dve.scalar_tensor_tensor(out=tot[:, k], in0=yk[1][:, k], scalar=w[:, k, 1:2], in1=acc[:, k], op0=ALU.mult, op1=ALU.add).then_inc(added, 1)
                for k in range(NBUF):
                    dve.wait_ge(added, m * NBUF + k + 1)
                    dve.bn_stats(stats[:, k], tot[:, k]).then_inc(stat_done, 1)
                dve.wait_ge(stat_done, (m + 1) * NBUF)
                dve.sem_inc(stat_seen, 1)
                for k in range(NBUF):
                    dve.bn_aggr(mv[:, k], stats[:, k]).then_inc(mean_done, 1)
                dve.wait_ge(std_done, m + 1)
                dve.reciprocal(rstd[:], std[:]).then_inc(rstd_done, 1)
                dve.wait_ge(rstd_done, m + 1)
                for k in range(NBUF):
                    dve.wait_ge(stored[k], m * 16)
                    dve.tensor_scalar(res[:, k], tot[:, k], mv[:, k, 0:1], rstd[:, k:k + 1], ALU.subtract, ALU.mult).then_inc(res_done, 1)


def laid_out(i):
    i = {k: np.asarray(v) for k, v in i.items()}
    x = i["L0_attn_hidden_states"]
    rep = lambda v: np.broadcast_to(v, (P, *v.shape))
    rel, gc = i["L0_attn_rel_embed"], i["L0_attn_gru_const"].reshape(H)
    stack = lambda e, f: np.concatenate([i[e], i[f][None]])
    a = {
        "x": x.reshape(T, E), "xt": x.transpose(0, 2, 1),
        "wq": i["L0_attn_Wq"].T, "wk": i["L0_attn_Wk"].T, "wv": i["L0_attn_Wv"].T, "wo": i["L0_attn_Wo"].T,
        "bq": i["L0_attn_bq"].reshape(EC, P).T, "bk": i["L0_attn_bk"].reshape(EC, P).T,
        "bv": rep(i["L0_attn_bv"]), "bo": rep(i["L0_attn_bo"]),
        "gru_w": np.tile(i["L0_attn_gru_W"].T, (P // D, 1)).reshape(P, 2, 4),
        "gru_b": rep(i["L0_attn_gru_b"].reshape(2, 4)),
        "gc_hj": np.repeat(gc, NI)[:, None], "gc_h": rep(gc),
        "rel": rel, "ends": rep(rel[[NEG, POS]]),
        "far_ends": np.repeat(rel[[NEG, POS]].T, NI, axis=0),
        "wr": i["L0_ffn_Wr"].T,
        "w1": stack("L0_ffn_W1", "L0_ffn_fw1"), "w2": stack("L0_ffn_W2", "L0_ffn_fw2"),
        "b1": stack("L0_ffn_b1", "L0_ffn_fb1").reshape(NE + 1, HC, P).transpose(0, 2, 1),
        "b2": stack("L0_ffn_b2", "L0_ffn_fb2"),
    }
    return {k: np.ascontiguousarray(v) for k, v in (a | shape_constants()).items()}


def kernel(**inputs):
    import concourse.bacc as _bacc
    from concourse.bass_utils import run_bass_kernel_spmd as _run

    nc = _bacc.Bacc("TRN2", target_bir_lowering=False, num_devices=1)
    arrays, args = {}, {}
    for name, v in laid_out(inputs).items():
        arrays[f"in_{name}"] = v
        args[name] = nc.dram_tensor(f"in_{name}", v.shape, mybir.dt.from_np(v.dtype), kind="ExternalInput").ap()
    out = nc.dram_tensor("out_dram", (T, E), F32, kind="ExternalOutput").ap()
    layer(nc, args, out)
    r = _run(nc, [arrays], core_ids=[0])
    return r.results[0]["out_dram"].reshape(B, N, E)
```

```python
import math
from contextlib import ExitStack, nullcontext

import numpy as np

import concourse.bass as bass
from concourse import mybir

P = 128
F32 = mybir.dt.float32
BF16 = mybir.dt.bfloat16
I32 = mybir.dt.int32
U32 = mybir.dt.uint32
ALU = mybir.AluOpType
ACT = mybir.ActivationFunctionType
AX = mybir.AxisListType

B, N, E = 8, 1024, 256
H, D = 16, 16
T = B * N
EC = E // P
HQ = 4
NI = N // P
NB, MAXD = 80, 200
NEG, POS = NB // 2 - 1, NB - 1
EPS = 1e-5
NE, TOPK, HID = 8, 2, 1024
CAP = max(int(1.25 * (T * TOPK / NE)), 4)
TT = T // P
RT = 512
SLOTS = NE * CAP
ROWS = SLOTS + T
HC = HID // P
ZW = 1024
NZ = SLOTS * E // P // ZW
NF = T * E // P // ZW
PIECES_Q = (0, 0, 1, 0, 2, 1)
PIECES_K = (0, 1, 0, 2, 0, 1)


def buckets(rel):
    nb = NB // 2
    a = np.abs(rel)
    big = np.log(np.maximum(a, 1).astype(np.float32) / np.float32(nb // 2)).astype(np.float32)
    big = (big / np.float32(math.log(MAXD / (nb // 2))) * np.float32(nb - nb // 2)).astype(np.float32)
    big = np.minimum((nb // 2 + big).astype(np.int32), nb - 1)
    return (rel > 0) * nb + np.where(a < nb // 2, a, big)


REACH = int(max(r for r in range(N) if buckets(np.array(-r)) != NEG)) + 1
BAND = 2 * REACH + P - 2
LINE = BAND + P - 1
LO = REACH - 1
assert LO < 2 * P and BAND - LO < 3 * P


def shape_constants():
    v = (np.arange(LINE) - LO - (P - 1))[::-1]
    c = {"c_onehot": (np.arange(NB)[:, None] == buckets(v)[None, :]).astype(np.float32)}
    hd, hj = np.arange(P) // D, np.arange(P) // NI
    c["c_mask_hj"] = np.stack([(hd[:, None] + 8 * k == hj[None, :]) for k in range(EC)]).astype(np.float32)
    c["c_mask_h"] = np.stack([(hd[:, None] + 8 * k == np.arange(H)[None, :]) for k in range(EC)]).astype(np.float32)
    j, i = (np.arange(P) % NI)[:, None], np.arange(NI)[None, :]
    c["c_far"] = np.stack([j - i <= -2, j - i >= 2]).astype(np.float32)
    ind = np.zeros((32, N), np.float32)
    for s in range(3):
        for b in range(NI):
            ind[8 * s + b, b * P:(b + 1) * P] = 1
    c["c_ind"] = ind
    c["c_ident"] = np.eye(P, dtype=np.float32)
    c["c_order"] = np.broadcast_to(np.arange(NE, dtype=np.float32) - NE, (P, NE))
    c["c_token"] = (SLOTS + np.arange(TT)[None, :] * P + np.arange(P)[:, None]).astype(np.float32)
    c["c_to_end"] = np.broadcast_to((TT - np.arange(TT)).astype(np.float32), (P, TT))
    c["c_before"] = (np.arange(P)[:, None] < np.arange(P)[None, :]).astype(np.float32)
    return c


def layer(nc, a, out):
    es = ExitStack()

    def dram(name, shape, dt):
        return nc.dram_tensor(name, shape, dt, kind="Internal").ap()

    line_d = dram("line_d", [H, LINE], F32)
    slab_d = dram("slab_d", [P, H, BAND], F32)
    q_d = dram("q_d", [3, B, E, N], BF16)
    k_d = dram("k_d", [3, B, E, N], BF16)
    far_d = dram("far_d", [3, B, P, N], BF16)
    v_d = dram("v_d", [T, 2 * E], F32)
    gate_d = dram("gate_d", [B, P, P], F32)
    ot_d = dram("ot_d", [HQ, B, P, N], F32)
    xg_d = dram("xg_d", [ROWS, E], F32)
    yg_d = dram("yg_d", [ROWS, E], F32)

    with es:
        def sem(name):
            return es.enter_context(nc.semaphore(name))

        def keep(name, shape, dt=F32):
            return es.enter_context(nc.sbuf_tensor(name, shape, dt))

        ident = keep("ident", [P, P])
        gate_w = keep("gate_w", [P, EC, 2, P])
        gate_wt = keep("gate_wt", [P, EC, 2, H])
        gate_bs = keep("gate_bs", [P, 2])
        far_c = keep("far_c", [P, NI])
        logits = keep("logits", [P, TT, NE])
        slot_s = keep("slot_s", [P, TT, TOPK], U32)
        slot_g = keep("slot_g", [P, TT, TOPK], U32)
        wgt = keep("wgt", [P, TT, TOPK])
        last_tiles = keep("last_tiles", [P, 1], I32)
        zero = keep("zero", [P, ZW])
        zeroed = sem("zeroed")
        setup(nc, a, line_d, slab_d, zero, ident, gate_w, gate_wt, gate_bs, far_c)
        project(nc, a, q_d, k_d, far_d, v_d, gate_d, gate_w, gate_wt, gate_bs, far_c)
        attend(nc, a, q_d, k_d, far_d, v_d, gate_d, slab_d, ot_d, ident, xg_d, yg_d, zero, zeroed)
        merge(nc, a, ot_d, xg_d, ident, logits)
        route(nc, a, xg_d, zeroed, logits, slot_s, slot_g, wgt, last_tiles)
        ffn(nc, a, xg_d, yg_d, ident, last_tiles)
        combine(nc, a, xg_d, yg_d, slot_g, wgt, out)


def setup(nc, a, line_d, slab_d, zero, ident, gate_w, gate_wt, gate_bs, far_c):
    with ExitStack() as es:
        def sb(name, shape, dt=F32):
            return es.enter_context(nc.sbuf_tensor(name, shape, dt))

        def sem(name):
            return es.enter_context(nc.semaphore(name))

        onehot = sb("onehot", [NB, LINE])
        rel = sb("rel", [NB, H])
        line = sb("line", [H, LINE])
        falling = sb("falling", [P, H, BAND])
        slab = sb("slab", [P, H, BAND])
        ends = sb("ends", [P, 2, H])
        far_ends = sb("far_ends", [P, 2])
        far_mask = sb("far_mask", [P, 2, NI])
        far_t = sb("far_t", [P, NI])
        gw = sb("gw", [P, 2, 4])
        gb = sb("gb", [P, 2, 4])
        wsum = sb("wsum", [P, 2])
        mask_hj = sb("mask_hj", [P, EC, P])
        mask_h = sb("mask_h", [P, EC, H])
        pl = es.enter_context(nc.psum_tensor("pl", [H, 2, 512], F32))
        loaded = sem("loaded")
        line_ready, line_copied, line_stored = sem("line_ready"), sem("line_copied"), sem("line_stored")
        slab_loaded, slab_ready, slab_stored = sem("slab_loaded"), sem("slab_ready"), sem("slab_stored")
        summed, far_part = sem("summed"), sem("far_part")
        small = [(onehot[:], a["c_onehot"]), (rel[:], a["rel"]), (gw[:], a["gru_w"]), (gb[:], a["gru_b"]),
                 (mask_hj[:], a["c_mask_hj"].rearrange("k p n -> p k n")),
                 (mask_h[:], a["c_mask_h"].rearrange("k p n -> p k n")),
                 (far_mask[:], a["c_far"].rearrange("k p n -> p k n")),
                 (ends[:], a["ends"]), (far_ends[:], a["far_ends"]), (ident[:], a["c_ident"])]
        block = es.enter_context(nc.Block())

        @block.sync
        def _(sp):
            with nc.allow_non_contiguous_dma(reason="small constants, once"):
                for to, of in small:
                    sp.dma_start(to, of).then_inc(loaded, 16)
            sp.wait_ge(line_copied, 1)
            sp.dma_start(line_d, line[:]).then_inc(line_stored, 16)
            sp.wait_ge(line_stored, 16)
            for h in range(H):
                skew = bass.AP(line_d.tensor, h * LINE, [[1, P], [1, BAND]])
                sp.dma_start(falling[:, h, :], skew).then_inc(slab_loaded, 16)
            sp.wait_ge(slab_ready, 3)
            sp.dma_start(slab_d, slab[:]).then_inc(slab_stored, 16)
            sp.wait_ge(slab_stored, 16)

        @block.tensor
        def _(pe):
            pe.wait_ge(loaded, 16 * len(small))
            for c, (lo, hi) in enumerate(((0, 512), (512, LINE))):
                pe.matmul(pl[:, c, 0:hi - lo], rel[:], onehot[:, lo:hi], start=True, stop=True).then_inc(line_ready, 1)

        @block.vector
        def _(dve):
            dve.memset(zero[:], 0.0)
            dve.wait_ge(loaded, 16 * len(small))
            dve.tensor_reduce(wsum[:], gw[:], AX.X, ALU.add).then_inc(summed, 1)
            dve.tensor_reduce(gate_bs[:], gb[:], AX.X, ALU.add)
            dve.wait_ge(summed, 1)
            for g in range(2):
                dve.tensor_scalar(gate_w[:, :, g, :], mask_hj[:], wsum[:, g:g + 1], None, ALU.mult)
                dve.tensor_scalar(gate_wt[:, :, g, :], mask_h[:], wsum[:, g:g + 1], None, ALU.mult)
            dve.tensor_scalar(far_t[:], far_mask[:, 0, :], far_ends[:, 0:1], None, ALU.mult).then_inc(far_part, 1)
            dve.wait_ge(far_part, 1)
            dve.scalar_tensor_tensor(out=far_c[:], in0=far_mask[:, 1, :], scalar=far_ends[:, 1:2], in1=far_t[:],
                                     op0=ALU.mult, op1=ALU.add)
            dve.wait_ge(line_ready, 2)
            dve.tensor_copy(line[:, 0:512], pl[:, 0, :])
            dve.tensor_copy(line[:, 512:LINE], pl[:, 1, 0:LINE - 512]).then_inc(line_copied, 1)
            dve.wait_ge(slab_loaded, 16 * H)
            dve.tensor_copy(slab[:], falling[:, :, ::-1]).then_inc(slab_ready, 1)
            dve.wait_ge(slab_ready, 1)
            for n, (lo, hi) in enumerate(((0, LO - P), (LO + 2 * P, BAND))):
                dve.tensor_tensor(slab[:, :, lo:hi], slab[:, :, lo:hi],
                                  ends[:, n, :].rearrange("p (h o) -> p h o", o=1).to_broadcast([P, H, hi - lo]),
                                  ALU.subtract).then_inc(slab_ready, 1)


def project(nc, a, q_d, k_d, far_d, v_d, gate_d, gate_w, gate_wt, gate_bs, far_c):
    HT = N // 2
    NU = 4
    NS = NU + 1
    STORES = NS + 1
    with ExitStack() as es:
        def sb(name, shape, dt=F32):
            return es.enter_context(nc.sbuf_tensor(name, shape, dt))

        def sem(name):
            return es.enter_context(nc.semaphore(name))

        w_qk = sb("w_qk", [P, 2, EC, E])
        b_qk = sb("b_qk", [P, 2, EC])
        w_v = sb("w_v", [P, EC, E])
        b_v = sb("b_v", [P, E])
        gc_hj = sb("gc_hj", [P, 1])
        gc_h = sb("gc_h", [P, H])
        xt = sb("xt", [P, 2, EC, HT])
        full = sb("full", [P, NS, HT])
        rest = sb("rest", [P, NS, HT])
        parts = sb("parts", [P, 2, NS, 3, HT], BF16)
        sig = sb("sig", [P, 2, HT])
        gmix = sb("gmix", [P, HT])
        gout = sb("gout", [P, HT])
        vt = sb("vt", [P, 2, 4, H, 2 * D])
        gsig = sb("gsig", [P, 2, 4, H])
        gt1 = sb("gt1", [P, 4, H])
        gt2 = sb("gt2", [P, 4, H])
        gtok = sb("gtok", [P, HQ, NI, 4])
        pu = es.enter_context(nc.psum_tensor("pu", [P, 4, 512], F32))
        pv = es.enter_context(nc.psum_tensor("pv", [P, 2, 2, E], F32))
        pg = es.enter_context(nc.psum_tensor("pg", [P, 4, 2, H], F32))
        loaded, x_loaded = sem("w_loaded"), [sem("x_loaded0"), sem("x_loaded1")]
        unit_done, qk_full, far_full = sem("unit_done"), sem("qk_full"), sem("far_full")
        high_done, rest_done, mid_done, low_done = (sem(x) for x in ("high_done", "rest_done", "mid_done", "low_done"))
        sig_done, mix_step = sem("sig_done"), sem("mix_step")
        v_done, v_read, v_set = sem("v_done"), sem("v_read"), sem("v_set")
        gl_done = [sem("gl_done0"), sem("gl_done1")]
        gl_read, g_step, gtok_done = sem("gl_read"), sem("g_step"), sem("gtok_done")
        stored = [sem("stored0"), sem("stored1")]
        g_stored = sem("g_stored")
        weights = [(w_qk[:, 0], a["wq"].rearrange("(c p) n -> p c n", p=P)), (w_qk[:, 1], a["wk"].rearrange("(c p) n -> p c n", p=P)),
                   (w_v[:], a["wv"].rearrange("(c p) n -> p c n", p=P)), (b_qk[:, 0], a["bq"]), (b_qk[:, 1], a["bk"]),
                   (b_v[:], a["bv"]), (gc_hj[:], a["gc_hj"]), (gc_h[:], a["gc_h"])]
        block = es.enter_context(nc.Block())

        @block.sync
        def _(sp):
            with nc.allow_non_contiguous_dma(reason="small weights, once"):
                for to, of in weights:
                    sp.dma_start(to, of).then_inc(loaded, 16)

            def load(b, s):
                sp.wait_ge(gl_done[s], b)
                sp.dma_start(xt[:, s], a["xt"][bass.ds(b, 1), :, s * HT:(s + 1) * HT].rearrange("o (c p) n -> p (o c) n", p=P)).then_inc(x_loaded[s], 16)

            def store(b, s):
                t0 = s * HT
                sp.wait_ge(low_done, (2 * b + s + 1) * NS)
                for u in range(NU):
                    rows = slice((u % 2) * P, (u % 2 + 1) * P)
                    sp.dma_start((q_d, k_d)[u // 2][:, bass.ds(b, 1), rows, t0:t0 + HT].rearrange("s o p n -> p (s o) n"), parts[:, s, u]).then_inc(stored[s], 16)
                sp.dma_start(far_d[:, bass.ds(b, 1), :, t0:t0 + HT].rearrange("s o p n -> p (s o) n"), parts[:, s, NU]).then_inc(stored[s], 16)
                sp.wait_ge(v_read, (2 * b + s + 1) * 4)
                sp.dma_start(v_d[bass.ds(b * N + t0, HT), :].rearrange("(k p) n -> p k n", p=P),
                             vt[:, s].rearrange("p k h d -> p k (h d)")).then_inc(stored[s], 16)
                if s == 1:
                    sp.wait_ge(gtok_done, 2 * b + 2)
                    sp.dma_start(gate_d[bass.ds(b, 1)].rearrange("o p n -> p (o n)"), gtok[:].rearrange("p a i h -> p (a i h)")).then_inc(g_stored, 16)

            load(0, 0)
            load(0, 1)
            with sp.Fori(0, B - 1) as b:
                for s in range(2):
                    store(b, s)
                    load(b + 1, s)
            store(B - 1, 0)
            store(B - 1, 1)
            for s in range(2):
                sp.wait_ge(stored[s], 16 * STORES * B)
            sp.wait_ge(g_stored, 16 * B)

        @block.gpsimd
        def _(pool):
            pool.memset(vt[:], 0.0).then_inc(v_set, 1)
            with pool.Fori(0, 2 * B, 2) as h0:
                for s in range(2):
                    for u in range(NS):
                        pool.wait_ge(mid_done, (h0 + s) * NS + u + 1)
                        pool.tensor_tensor(parts[:, s, u, 2, :], rest[:, u, :], parts[:, s, u, 1, :], ALU.subtract).then_inc(low_done, 1)

        @block.tensor
        def _(pe):
            pe.wait_ge(loaded, 16 * len(weights))
            with pe.Fori(0, B) as b:
                for s in range(2):
                    h = 2 * b + s
                    pe.wait_ge(x_loaded[s], 16 * (b + 1))
                    for u in range(NU + 2):
                        if u < 2:
                            pe.wait_ge(sig_done, 2 * h)
                        elif u < NU:
                            pe.wait_ge(qk_full, NU * h)
                        else:
                            pe.wait_ge(qk_full, NU * h + u - NU + 1)
                        w = w_qk[:, u // 2, :, (u % 2) * P:(u % 2 + 1) * P] if u < NU else gate_w[:, :, u - NU, :]
                        for c in range(EC):
                            mm = pe.matmul(pu[:, u % 4, :], w[:, c, :], xt[:, s, c, :], start=c == 0, stop=c == EC - 1)
                        mm.then_inc(unit_done, 1)
                    pe.wait_ge(v_read, 4 * h)
                    for t in range(4):
                        for c in range(EC):
                            mm = pe.matmul(pv[:, t // 2, t % 2, :], xt[:, s, c, t * P:(t + 1) * P], w_v[:, c, :], start=c == 0, stop=c == EC - 1)
                        if t % 2 == 1:
                            mm.then_inc(v_done, 1)
                    pe.wait_ge(gl_read, 2 * h)
                    for t in range(4):
                        for c in range(EC):
                            mm = pe.matmul(pg[:, t].rearrange("p g h -> p (g h)"), xt[:, s, c, t * P:(t + 1) * P],
                                           gate_wt[:, c].rearrange("p g h -> p (g h)"), start=c == 0, stop=c == EC - 1)
                    mm.then_inc(gl_done[s], 1)

        @block.scalar
        def _(act):
            act.wait_ge(loaded, 16 * len(weights))
            with act.Fori(0, B) as b:
                for s in range(2):
                    h = 2 * b + s

                    def middle(u):
                        act.wait_ge(rest_done, h * NS + u + 1)
                        act.activation(parts[:, s, u, 1, :], rest[:, u, :], ACT.Copy).then_inc(mid_done, 1)

                    act.wait_ge(stored[s], 16 * STORES * b)
                    for u in range(NU):
                        act.wait_ge(qk_full, h * NU + u + 1)
                        act.activation(parts[:, s, u, 0, :], full[:, u, :], ACT.Copy).then_inc(high_done, 1)
                        if u > 0:
                            middle(u - 1)
                    middle(NU - 1)
                    act.wait_ge(mix_step, 2 * h)
                    for g in range(2):
                        act.wait_ge(unit_done, h * (NU + 2) + NU + g + 1)
                        act.activation(sig[:, g, :], pu[:, g, :], ACT.Sigmoid, bias=gate_bs[:, g:g + 1]).then_inc(sig_done, 1)
                    act.wait_ge(gl_done[s], b + 1)
                    act.wait_ge(g_step, 2 * h)
                    for g in range(2):
                        act.activation(gsig[:, g], pg[:, :, g, :], ACT.Sigmoid, bias=gate_bs[:, g:g + 1]).then_inc(gl_read, 1)
                    act.wait_ge(far_full, h + 1)
                    act.activation(parts[:, s, NU, 0, :], full[:, NU, :], ACT.Copy).then_inc(high_done, 1)
                    middle(NU)

        @block.vector
        def _(dve):
            dve.wait_ge(loaded, 16 * len(weights))
            dve.wait_ge(v_set, 1)
            with dve.Fori(0, B) as b:
                for s in range(2):
                    h = 2 * b + s

                    def rest_of(u):
                        dve.wait_ge(high_done, h * NS + u + 1)
                        dve.tensor_tensor(rest[:, u, :], full[:, u, :], parts[:, s, u, 0, :], ALU.subtract).then_inc(rest_done, 1)

                    dve.wait_ge(low_done, h * NS)
                    for u in range(NU):
                        dve.wait_ge(unit_done, h * (NU + 2) + u + 1)
                        scale = 1.0 / math.sqrt(D) if u < 2 else 1.0
                        dve.tensor_scalar(full[:, u, :], pu[:, u, :], b_qk[:, u // 2, u % 2:u % 2 + 1], scale, ALU.add, ALU.mult).then_inc(qk_full, 1)
                        if u > 0:
                            rest_of(u - 1)
                    rest_of(NU - 1)
                    dve.wait_ge(stored[s], 16 * STORES * b)
                    for t in range(4):
                        dve.wait_ge(v_done, 2 * h + t // 2 + 1)
                        dve.tensor_tensor(vt[:, s, t, :, 0:D], pv[:, t // 2, t % 2, :].rearrange("p (h d) -> p h d", d=D),
                                          b_v[:].rearrange("p (h d) -> p h d", d=D), ALU.add).then_inc(v_read, 1)
                    dve.wait_ge(sig_done, 2 * h + 2)
                    dve.tensor_scalar(gmix[:], sig[:, 1, :], gc_hj[:, 0:1], -1.0, ALU.mult, ALU.add).then_inc(mix_step, 1)
                    dve.wait_ge(mix_step, 2 * h + 1)
                    dve.tensor_tensor(gout[:], sig[:, 0, :], gmix[:], ALU.mult).then_inc(mix_step, 1)
                    dve.wait_ge(mix_step, 2 * h + 2)
                    for i in range(4):
                        ins = dve.tensor_scalar(full[:, NU, i * P:(i + 1) * P], gout[:, i * P:(i + 1) * P], 2.0,
                                                far_c[:, 4 * s + i:4 * s + i + 1], ALU.add, ALU.mult)
                    ins.then_inc(far_full, 1)
                    dve.wait_ge(gl_read, 2 * h + 2)
                    dve.tensor_tensor(gt1[:], gsig[:, 1], gc_h[:].rearrange("p (o h) -> p o h", o=1).to_broadcast([P, 4, H]), ALU.mult).then_inc(g_step, 1)
                    dve.wait_ge(g_step, 2 * h + 1)
                    dve.scalar_tensor_tensor(out=gt2[:], in0=gt1[:], scalar=-1.0, in1=gsig[:, 0], op0=ALU.add, op1=ALU.mult).then_inc(g_step, 1)
                    dve.wait_ge(g_step, 2 * h + 2)
                    if s == 0:
                        dve.wait_ge(g_stored, 16 * b)
                    for i in range(4):
                        ins = dve.tensor_scalar(gtok[:, :, 4 * s + i, :], gt2[:, i, :].rearrange("p (a h) -> p a h", h=4), 2.0, None, ALU.add)
                    ins.then_inc(gtok_done, 1)
                    rest_of(NU)


SIDE = (NI - 1) * P - LO
WIDE = SIDE + N + LO


def window(i):
    return SIDE - (i * P - LO)


def attend(nc, a, q_d, k_d, far_d, v_d, gate_d, slab_d, ot_d, ident, xg_d, yg_d, zero, zeroed):
    R = NI * 4
    STEPS = 4
    BODIES = B // STEPS
    with ExitStack() as es:
        def sb(name, shape, dt=F32):
            return es.enter_context(nc.sbuf_tensor(name, shape, dt))

        def sem(name):
            return es.enter_context(nc.semaphore(name))

        qs = [sb(f"qs{k}", [P, 4, N], BF16) for k in range(2)]
        ks = [sb(f"ks{k}", [P, 4, N], BF16) for k in range(2)]
        vs = [sb(f"vs{k}", [P, NI, P]) for k in range(2)]
        gs = [sb(f"gs{k}", [P, NI, 4]) for k in range(2)]
        slab = sb("slab_a", [P, 4, BAND])
        ind = sb("ind", [P, N])
        gbias = [sb(f"gbias{k}", [P, WIDE]) for k in range(4)]
        probs = sb("probs", [P, 2, N])
        pts = sb("pts", [P, 2, 4, NI, P])
        negm = sb("negm", [P, 4])
        sums = sb("sums", [P, 2, 4])
        rsum = sb("rsum", [P, 2, 4])
        rs = sb("rs", [P, 2, 4, 32])
        rsb = sb("rsb", [P, P])
        ot = sb("ot", [P, 2, N])
        sc = es.enter_context(nc.psum_tensor("sc", [P, 2, N], F32))
        pt = es.enter_context(nc.psum_tensor("pt", [P, 3, 4, P], F32))
        pop = es.enter_context(nc.psum_tensor("pop", [P, 2, 256], F32))
        po, pr = pop[:, 0, 0:P], pop[:, 1, 0:P]
        zeros_set, gbias_done, waited, pool_waited = (sem(x) for x in ("zeros_set", "gbias_done", "waited", "pool_waited"))
        ind_in, consts_set = sem("ind_in"), sem("consts_set")
        in_ready = [sem("in_ready0"), sem("in_ready1")]
        slab_in = sem("slab_in")
        scores_done, max_done, exp_done = (sem(x) for x in ("scores_done", "max_done", "exp_done"))
        tr_done = sem("tr_done")
        copied_a, copied_v = sem("copied_a"), sem("copied_v")
        av_done, recip_done, rs_done, rcopied = (sem(x) for x in ("av_done", "recip_done", "rs_done", "rcopied"))
        ot_done = [sem("ot_done0"), sem("ot_done1")]
        ot_stored = [sem("ot_stored0"), sem("ot_stored1")]
        LOADS = 17
        block = es.enter_context(nc.Block())

        def by_scalar(r, half):
            return half == 0 or r % 4 == 0

        def halves(r, half):
            n = [by_scalar(x // 2, x % 2) for x in range(2 * r + half + 1)]
            return sum(n), len(n) - sum(n)

        def bank(k, r, half):
            return ((k * R + r) * 2 + half) % 3

        slots_flat = xg_d[0:SLOTS, :].rearrange("(p r) e -> p (r e)", p=P)
        fallback_flat = yg_d[SLOTS:ROWS, :].rearrange("(p r) e -> p (r e)", p=P)
        assert NZ % (HQ * BODIES) == 0 and NF % (HQ * BODIES) == 0
        SA, SV = halves(R - 1, 1)
        rows = [(k, r) for k in range(STEPS) for r in range(R)]

        def uses(body, k):
            return body * (STEPS // 2) + k // 2

        def blocks_before(m, k, i):
            return m * NI + (i - 1 if i > 0 or k > 0 else 0)

        @block.sync
        def _(sp):
            sp.dma_start(ind[96:128, :], a["c_ind"]).then_inc(ind_in, 16)
            sp.wait_ge(consts_set, 10)
            with sp.Fori(0, HQ) as g:
                with sp.Fori(0, BODIES) as bb:
                    body = sp.snap(g * BODIES + bb)
                    for k in range(STEPS):
                        b = bb * STEPS + k
                        kk = k % 2
                        if k == 1:
                            sp.wait_ge(gbias_done, body * (STEPS * R))
                            sp.dma_start(slab[:], slab_d[:, bass.ds(g * 4, 4), :]).then_inc(slab_in, 16)
                        sp.wait_ge(ot_done[kk], uses(body, k) * NI)
                        for s in range(6):
                            sp.dma_start(ks[kk][D * s:D * s + D], k_d[PIECES_K[s], bass.ds(b, 1), bass.ds(g * 64, 64), :].rearrange("o (h d) n -> d (o h) n", d=D)).then_inc(in_ready[kk], 16)
                            sp.dma_start(qs[kk][D * s:D * s + D], q_d[PIECES_Q[s], bass.ds(b, 1), bass.ds(g * 64, 64), :].rearrange("o (h d) n -> d (o h) n", d=D)).then_inc(in_ready[kk], 16)
                        for s in range(3):
                            sp.dma_start(qs[kk][96 + 8 * s:104 + 8 * s], far_d[s, bass.ds(b, 1), bass.ds(g * 32, 32), :].rearrange("o (h j) n -> j (o h) n", j=NI)).then_inc(in_ready[kk], 16)
                        sp.dma_start(vs[kk][:], v_d[bass.ds(b * N, N), bass.ds(g * P, P)].rearrange("(j p) n -> p j n", p=P)).then_inc(in_ready[kk], 16)
                        sp.dma_start(gs[kk][:].rearrange("p i h -> p (i h)"), gate_d[bass.ds(b, 1), :, bass.ds(g * 32, 32)].rearrange("o p n -> p (o n)")).then_inc(in_ready[kk], 16)
                    for flat, n in ((slots_flat, NZ), (fallback_flat, NF)):
                        n //= HQ * BODIES
                        for c in range(n):
                            sp.dma_start(flat[:, bass.ds(body * (n * ZW) + c * ZW, ZW)], zero[:]).then_inc(zeroed, 16)

        @block.gpsimd
        def _(pool):
            for t in gbias:
                pool.memset(t[:], 0.0).then_inc(zeros_set, 1)
            pool.wait_ge(zeros_set, 4)
            with pool.Fori(0, HQ) as g:
                with pool.Fori(0, BODIES) as bb:
                    body = pool.snap(g * BODIES + bb)
                    for k in range(STEPS):
                        pool.wait_ge(in_ready[k % 2], (uses(body, k) + 1) * (16 * LOADS))
                        if k == 0:
                            pool.wait_ge(slab_in, (body + 1) * 16)
                        for r in range(R):
                            m = body * STEPS + k
                            pool.wait_ge(max_done, m * R + (r - 3 if k > 0 or r > 3 else 0))
                            pool.sem_inc(pool_waited, 1)
                            pool.tensor_scalar(gbias[r % 4][:, SIDE:SIDE + BAND], slab[:, r % 4, :], gs[k % 2][:, r // 4, r % 4:r % 4 + 1], 1.0,
                                               ALU.mult, ALU.mult).then_inc(gbias_done, 1)

        @block.tensor
        def _(pe):
            pe.wait_ge(consts_set, 10)
            with pe.Fori(0, HQ) as g:
                with pe.Fori(0, BODIES) as bb:
                    body = pe.snap(g * BODIES + bb)

                    def scores(k, r):
                        i, hh = r // 4, r % 4
                        if r == 0:
                            pe.wait_ge(in_ready[k % 2], (uses(body, k) + 1) * (16 * LOADS))
                        for c in range(2):
                            mm = pe.matmul(sc[:, r % 2, c * 512:(c + 1) * 512], qs[k % 2][:, hh, i * P:(i + 1) * P],
                                           ks[k % 2][:, hh, c * 512:(c + 1) * 512], start=True, stop=True)
                        mm.then_inc(scores_done, 1)

                    def turn(k, r):
                        m = body * STEPS + k
                        for half in range(2):
                            q = (k * R + r) * 2 + half - 3
                            if q >= 0:
                                k0, h0 = q // (2 * R), q % (2 * R)
                                na, nv = halves(h0 // 2, h0 % 2)
                                if by_scalar(h0 // 2, h0 % 2):
                                    pe.wait_ge(copied_a, (body * STEPS + k0) * SA + na)
                                else:
                                    pe.wait_ge(copied_v, (body * STEPS + k0) * SV + nv)
                            for j in range(4):
                                jj = 4 * half + j
                                mm = pe.transpose(pt[:, bank(k, r, half), j, :], probs[:, r % 2, jj * P:(jj + 1) * P], ident[:])
                            mm.then_inc(tr_done, 1)

                    def weigh(k, i, part):
                        m = body * STEPS + k
                        if part == 0:
                            na, nv = halves(4 * i + 3, 1)
                            pe.wait_ge(copied_a, m * SA + na)
                            pe.wait_ge(copied_v, m * SV + nv)
                            if i > 0:
                                pe.wait_ge(ot_done[k % 2], uses(body, k) * NI + i)
                            else:
                                pe.wait_ge(ot_done[(k + 1) % 2], uses(body, k + 1) * NI)
                        for j in range(3 * part, min(3 * part + 3, NI)):
                            for hh in range(4):
                                mm = pe.matmul(po[32 * hh:32 * hh + 32], vs[k % 2][:, j, 32 * hh:32 * hh + 32], pts[:, i % 2, hh, j, :],
                                               start=j == 0, stop=j == NI - 1, skip_group_check=True)
                        if part == 2:
                            pe.wait_ge(rs_done, m * NI + i + 1)
                            pe.transpose(pr, rs[:, i % 2, :, :].rearrange("p h o -> p (h o)"), ident[:]).then_inc(av_done, 1)

                    scores(*rows[0])
                    scores(*rows[1])
                    for x in range(len(rows) + 4):
                        if x < len(rows):
                            pe.wait_ge(exp_done, (body * STEPS + rows[x][0]) * R + rows[x][1] + 1)
                            if x + 2 < len(rows):
                                scores(*rows[x + 2])
                            turn(*rows[x])
                        if x >= 4:
                            k, r = rows[x - 4]
                            if r % 4 < 3:
                                weigh(k, r // 4, r % 4)

        @block.vector
        def _(dve):
            for k in range(2):
                dve.memset(qs[k][96:128], 0.0).then_inc(consts_set, 1)
            dve.wait_ge(ind_in, 16)
            for k in range(2):
                for hh in range(4):
                    dve.tensor_copy(ks[k][96:128, hh, :], ind[96:128, :]).then_inc(consts_set, 1)
            with dve.Fori(0, HQ) as g:
                with dve.Fori(0, BODIES) as bb:
                    body = dve.snap(g * BODIES + bb)

                    def bias_and_max(k, r):
                        m = body * STEPS + k
                        dve.wait_ge(gbias_done, m * R + r + 1)
                        dve.wait_ge(scores_done, m * R + r + 1)
                        dve.sem_inc(waited, 1)
                        w = window(r // 4)
                        dve.tensor_tensor_reduce(sc[:, r % 2, :], sc[:, r % 2, :], gbias[r % 4][:, w:w + N], -1.0, 3.0e38,
                                                 ALU.add, ALU.min, negm[:, r % 4:r % 4 + 1]).then_inc(max_done, 1)

                    def copy_out(k, r):
                        m = body * STEPS + k
                        i, hh = r // 4, r % 4
                        if not by_scalar(r, 1):
                            dve.wait_ge(tr_done, (m * R + r + 1) * 2)
                            if hh == 1:
                                dve.wait_ge(av_done, blocks_before(m, k, i))
                            dve.tensor_copy(pts[:, i % 2, hh, 4:8, :], pt[:, bank(k, r, 1)]).then_inc(copied_v, 1)

                    def reciprocals(k, i):
                        m = body * STEPS + k
                        dve.wait_ge(exp_done, m * R + 4 * i + 4)
                        dve.reciprocal(rsum[:, i % 2, :], sums[:, i % 2, :]).then_inc(recip_done, 1)
                        dve.wait_ge(recip_done, m * NI + i + 1)
                        dve.wait_ge(av_done, blocks_before(m, k, i))
                        dve.tensor_copy(rs[:, i % 2], rsum[:, i % 2, :].rearrange("p (h o) -> p h o", o=1).to_broadcast([P, 4, 32])).then_inc(rs_done, 1)

                    def finish(k, i):
                        m = body * STEPS + k
                        if i == 0:
                            dve.wait_ge(ot_stored[k % 2], uses(body, k) * 16)
                        dve.wait_ge(rcopied, m * NI + i + 1)
                        dve.wait_ge(av_done, m * NI + i + 1)
                        dve.tensor_tensor(ot[:, k % 2, i * P:(i + 1) * P], po, rsb[:], ALU.mult).then_inc(ot_done[k % 2], 1)

                    for x in range(len(rows) + 6):
                        if x < len(rows):
                            bias_and_max(*rows[x])
                        if x >= 6 and rows[x - 6][1] % 4 == 3:
                            finish(rows[x - 6][0], rows[x - 6][1] // 4)
                        if 2 <= x <= len(rows) + 1:
                            k, r = rows[x - 2]
                            copy_out(k, r)
                            if r % 4 == 3:
                                reciprocals(k, r // 4)

        @block.scalar
        def _(act):
            with act.Fori(0, HQ) as g:
                with act.Fori(0, BODIES) as bb:
                    body = act.snap(g * BODIES + bb)

                    def exponential(k, r):
                        m = body * STEPS + k
                        i, hh = r // 4, r % 4
                        act.wait_ge(max_done, m * R + r + 1)
                        if k > 0 or r >= 2:
                            act.wait_ge(tr_done, (m * R + r - 1) * 2)
                        if hh == 0:
                            act.wait_ge(rs_done, blocks_before(m, k, i))
                        act.activation(probs[:, r % 2, :], sc[:, r % 2, :], ACT.Exp, bias=negm[:, r % 4:r % 4 + 1], scale=-1.0,
                                       accum_out=sums[:, i % 2, hh:hh + 1]).then_inc(exp_done, 1)

                    def copy_out(k, r):
                        m = body * STEPS + k
                        i, hh = r // 4, r % 4
                        for half in range(2):
                            if by_scalar(r, half):
                                act.wait_ge(tr_done, (m * R + r) * 2 + half + 1)
                                if hh == 0 and half == 0:
                                    act.wait_ge(av_done, blocks_before(m, k, i))
                                act.activation(pts[:, i % 2, hh, 4 * half:4 * half + 4, :], pt[:, bank(k, r, half)], ACT.Copy).then_inc(copied_a, 1)

                    def copy_sums(k, i):
                        m = body * STEPS + k
                        act.wait_ge(av_done, m * NI + i + 1)
                        act.activation(rsb[:], pr, ACT.Copy).then_inc(rcopied, 1)

                    def store(k):
                        act.wait_ge(ot_done[k % 2], (uses(body, k) + 1) * NI)
                        act.dma_start(ot_d[bass.ds(g, 1), bass.ds(bb * STEPS + k, 1)].rearrange("o w p n -> p (o w n)"), ot[:, k % 2, :]).then_inc(ot_stored[k % 2], 16)

                    for x in range(len(rows) + 5):
                        if x > R and x % R == 10:
                            store(x // R - 1)
                        if x < len(rows):
                            exponential(*rows[x])
                        if x >= 5 and rows[x - 5][1] % 4 == 3:
                            copy_sums(rows[x - 5][0], rows[x - 5][1] // 4)
                        if 1 <= x <= len(rows):
                            copy_out(*rows[x - 1])
                    store(STEPS - 1)
            for k in range(2):
                act.wait_ge(ot_stored[k], 16 * HQ * B // 2)


def merge(nc, a, ot_d, xg_d, ident, logits):
    with ExitStack() as es:
        def sb(name, shape, dt=F32):
            return es.enter_context(nc.sbuf_tensor(name, shape, dt))

        def sem(name):
            return es.enter_context(nc.semaphore(name))

        TC = 2
        NCH = NI // TC
        w_o = sb("w_o", [P, HQ, E])
        b_o = sb("b_o", [P, E])
        w_r = sb("w_r", [P, EC, NE])
        otl = sb("otl", [P, 2, HQ, TC * P])
        xr = sb("xr", [P, 2, TC, E])
        xb = sb("xb", [P, 2, TC, E])
        y = sb("y", [P, 2, E])
        stats = sb("stats", [P, TC, 6])
        mv = sb("mv", [P, TC, 2])
        std = sb("std", [P, TC])
        rstd = sb("rstd", [P, TC])
        eps = sb("eps", [P, 1])
        x1 = sb("x1", [P, 2, E])
        x1t = sb("x1t", [P, 2, E])
        py = es.enter_context(nc.psum_tensor("py", [P, 2, 512], F32))
        px = es.enter_context(nc.psum_tensor("px", [P, 2, 512], F32))
        pl = es.enter_context(nc.psum_tensor("plg", [P, 2, 512], F32))
        loaded, w_zero = sem("mw_loaded"), sem("w_zero")
        in_ready = [sem("m_in0"), sem("m_in1")]
        y_done, x_biased, added, stat_done, mean_done, std_done, rstd_done, x1_done = (
            sem("m_" + n) for n in ("y_done", "x_biased", "added", "stat_done", "mean_done", "std_done", "rstd_done", "x1_done"))
        turned, turned_out, routed, logits_out = (sem("m_" + n) for n in ("turned", "turned_out", "routed", "logits_out"))
        x1_stored = [sem("x1_stored0"), sem("x1_stored1")]
        stat_seen = sem("m_stat_seen")
        tiles = [(c, t) for c in range(NCH) for t in range(TC)]
        block = es.enter_context(nc.Block())

        @block.sync
        def _(sp):
            with nc.allow_non_contiguous_dma(reason="small weights, once"):
                sp.dma_start(b_o[:], a["bo"]).then_inc(loaded, 16)
                sp.dma_start(w_r[:], a["wr"].rearrange("(c p) n -> p c n", p=P)).then_inc(loaded, 16)
            sp.wait_ge(w_zero, 1)
            for h in range(4):
                sp.dma_start(w_o[32 * h:32 * h + D], a["wo"].rearrange("(g h d) n -> h d g n", h=4, d=D)[h]).then_inc(loaded, 16)
            with sp.Fori(0, B) as b:
                for c in range(NCH):
                    sp.wait_ge(added, b * NI + (c - 1) * TC if c > 0 else b * NI)
                    sp.dma_start(otl[:, c % 2], ot_d[:, bass.ds(b, 1), :, c * TC * P:(c + 1) * TC * P].rearrange("g o p n -> p (g o) n")).then_inc(in_ready[c % 2], 16)
                    sp.dma_start(xr[:, c % 2], a["x"][bass.ds(b * N + c * TC * P, TC * P), :].rearrange("(t p) n -> p t n", p=P)).then_inc(in_ready[c % 2], 16)

        @block.gpsimd
        def _(pool):
            pool.memset(w_o[:], 0.0).then_inc(w_zero, 1)
            pool.memset(eps[:], EPS).then_inc(w_zero, 1)
            pool.wait_ge(loaded, 16 * 6)
            with pool.Fori(0, B) as b:
                for c in range(NCH):
                    q = b * (NCH // 2) + c // 2
                    pool.wait_ge(in_ready[c % 2], (q + 1) * 32)
                    pool.wait_ge(added, b * NI + (c - 1) * TC if c > 0 else b * NI)
                    for t in range(TC):
                        pool.tensor_tensor(xb[:, c % 2, t], xr[:, c % 2, t], b_o[:], ALU.add).then_inc(x_biased, 1)
                    for t in range(TC):
                        n = c * TC + t
                        pool.wait_ge(x1_done, b * NI + n + 1)
                        pool.dma_start(xg_d[bass.ds(b * N + SLOTS + n * P, P), :], x1[:, n % 2]).then_inc(x1_stored[n % 2], 16)
            for k in range(2):
                pool.wait_ge(x1_stored[k], 16 * TT // 2)

        @block.tensor
        def _(pe):
            pe.wait_ge(loaded, 16 * 6)
            with pe.Fori(0, B) as b:
                def project_out(c, t):
                    n = c * TC + t
                    if t == 0:
                        pe.wait_ge(in_ready[c % 2], (b * (NCH // 2) + c // 2 + 1) * 32)
                    if n >= 2:
                        pe.wait_ge(added, b * NI + n - 1)
                    for g in range(HQ):
                        mm = pe.matmul(py[:, n % 2, 0:E], otl[:, c % 2, g, t * P:(t + 1) * P], w_o[:, g, :], start=g == 0, stop=g == HQ - 1)
                    mm.then_inc(y_done, 1)

                def turn_and_route(n):
                    pe.wait_ge(x1_done, b * NI + n + 1)
                    if n >= 2:
                        pe.wait_ge(turned_out, b * NI + n - 1)
                    for k in range(EC):
                        mm = pe.transpose(px[:, n % 2, k * P:(k + 1) * P], x1[:, n % 2, k * P:(k + 1) * P], ident[:])
                    mm.then_inc(turned, 1)
                    pe.wait_ge(turned_out, b * NI + n + 1)
                    pe.wait_ge(logits_out, b * NI + max(n - 1, 0))
                    for k in range(EC):
                        mm = pe.matmul(pl[:, n % 2, 0:NE], x1t[:, n % 2, k * P:(k + 1) * P], w_r[:, k, :], start=k == 0, stop=k == EC - 1)
                    mm.then_inc(routed, 1)

                project_out(*tiles[0])
                project_out(*tiles[1])
                for n in range(NI):
                    if n % TC == 0:
                        for t in range(TC):
                            if n + TC + t < NI:
                                project_out(*tiles[n + TC + t])
                    turn_and_route(n)

        @block.scalar
        def _(act):
            act.wait_ge(w_zero, 2)
            with act.Fori(0, B) as b:
                for c in range(NCH):
                    act.wait_ge(mean_done, b * NI + (c + 1) * TC)
                    act.activation(std[:], mv[:, :, 1], ACT.Sqrt, bias=eps[:, 0:1]).then_inc(std_done, 1)
                    for t in range(TC):
                        n = c * TC + t
                        act.wait_ge(turned, b * NI + n + 1)
                        act.activation(x1t[:, n % 2], px[:, n % 2, 0:E], ACT.Copy).then_inc(turned_out, 1)

        @block.vector
        def _(dve):
            with dve.Fori(0, B) as b:
                def logits_out_of(c):
                    for t in range(TC):
                        n = c * TC + t
                        dve.wait_ge(routed, b * NI + n + 1)
                        dve.tensor_copy(logits[:, bass.ds(b * NI + n, 1), :], pl[:, t:t + 1, 0:NE]).then_inc(logits_out, 1)

                for c in range(NCH):
                    n0 = b * NI + c * TC
                    for t in range(TC):
                        dve.wait_ge(y_done, n0 + t + 1)
                        dve.wait_ge(x_biased, n0 + t + 1)
                        dve.tensor_tensor(y[:, t], py[:, t, 0:E], xb[:, c % 2, t], ALU.add).then_inc(added, 1)
                    for t in range(TC):
                        dve.wait_ge(added, n0 + t + 1)
                        dve.bn_stats(stats[:, t], y[:, t]).then_inc(stat_done, 1)
                    dve.wait_ge(stat_done, n0 + TC)
                    dve.sem_inc(stat_seen, 1)
                    for t in range(TC):
                        dve.bn_aggr(mv[:, t], stats[:, t]).then_inc(mean_done, 1)
                    if c > 0:
                        logits_out_of(c - 1)
                    dve.wait_ge(std_done, b * NCH + c + 1)
                    dve.reciprocal(rstd[:], std[:]).then_inc(rstd_done, 1)
                    dve.wait_ge(rstd_done, b * NCH + c + 1)
                    for t in range(TC):
                        dve.wait_ge(x1_stored[t], (b * NCH + c) * 16)
                        if c > 0:
                            dve.wait_ge(turned, b * NI + (c - 1) * TC + t + 1)
                        dve.tensor_scalar(x1[:, t], y[:, t], mv[:, t, 0:1], rstd[:, t:t + 1], ALU.subtract, ALU.mult).then_inc(x1_done, 1)
                logits_out_of(NCH - 1)


def route(nc, a, xg_d, zeroed, logits, slot_s, slot_g, wgt, last_tiles):
    with ExitStack() as es:
        def sb(name, shape, dt=F32):
            return es.enter_context(nc.sbuf_tensor(name, shape, dt))

        def sem(name):
            return es.enter_context(nc.semaphore(name))

        wide = [P, TT, NE]
        lz, pr, oh1, oh2, tmp, taken = (sb("r_" + n, wide) for n in ("lz", "pr", "oh1", "oh2", "tmp", "taken"))
        m1, m2, s1, s2, best, nfb, elig, incl, pos, kept, over, ones, fbm = (
            sb("r_" + n, [P, TT]) for n in ("m1", "m2", "s1", "s2", "best", "nfb", "elig", "incl", "pos", "kept", "over", "ones", "fbm"))
        order = sb("r_order", [P, NE])
        token = sb("r_token", [P, TT])
        to_end = sb("r_to_end", [P, TT])
        most = sb("r_most", [P, 1])
        before = sb("r_before", [P, P])
        all1 = sb("r_all1", [P, P])
        NBUF = 4
        xs = sb("r_xs", [P, NBUF, E])
        idx = sb("r_idx", [P, NBUF, TOPK], U32)
        pp = es.enter_context(nc.psum_tensor("r_pp", [P, 2, 512], F32))
        loaded, step, shifted, exped, elig_done, counted, slots_done = (
            sem("r_" + n) for n in ("loaded", "step", "shifted", "exped", "elig_done", "counted", "slots_done"))
        xs_in = [sem(f"r_xs{k}") for k in range(NBUF)]
        idx_set, idx_seen = sem("r_idx_set"), sem("r_idx_seen")
        away_done = sem("r_away_done")
        scattered = [sem(f"r_sc{k}") for k in range(NBUF)]
        block = es.enter_context(nc.Block())

        def over_experts(x):
            return x.rearrange("p (t o) -> p t o", o=1).to_broadcast(wide)

        def over_tiles(x):
            return x.rearrange("p (o e) -> p o e", o=1).to_broadcast(wide)

        @block.sync
        def _(sp):
            sp.dma_start(order[:], a["c_order"]).then_inc(loaded, 16)
            sp.dma_start(token[:], a["c_token"]).then_inc(loaded, 16)
            sp.dma_start(before[:], a["c_before"]).then_inc(loaded, 16)
            sp.dma_start(to_end[:], a["c_to_end"]).then_inc(loaded, 16)
            with sp.Fori(0, TT // NBUF) as m:
                for k in range(NBUF):
                    sp.wait_ge(scattered[k], m * 32)
                    sp.dma_start(xs[:, k], xg_d[bass.ds(m * (NBUF * P) + SLOTS + k * P, P), :]).then_inc(xs_in[k], 16)

        @block.scalar
        def _(act):
            act.wait_ge(shifted, 1)
            act.activation(lz[:], lz[:], ACT.Exp).then_inc(exped, 1)

        @block.tensor
        def _(pe):
            pe.wait_ge(loaded, 64)
            for e in range(NE):
                pe.wait_ge(elig_done, e + 2)
                pe.matmul(pp[:, 0, 0:TT], before[:], elig[:], start=True, stop=True)
                pe.matmul(pp[:, 1, 0:TT], all1[:], elig[:], start=True, stop=True).then_inc(counted, 1)
            pe.wait_ge(away_done, 1)
            pe.matmul(pp[:, 1, 0:TT], all1[:], fbm[:], start=True, stop=True).then_inc(counted, 1)

        @block.vector
        def _(dve):
            chain = [0]

            def then(ins):
                chain[0] += 1
                ins.then_inc(step, 1)
                dve.wait_ge(step, chain[0])

            dve.wait_ge(loaded, 64)
            dve.memset(all1[:], 1.0)
            dve.memset(ones[:], 1.0)
            dve.memset(nfb[:], 1.0).then_inc(elig_done, 1)
            then(dve.tensor_reduce(m1[:], logits[:], AX.X, ALU.max))
            dve.tensor_tensor(lz[:], logits[:], over_experts(m1[:]), ALU.subtract).then_inc(shifted, 1)
            dve.wait_ge(exped, 1)
            then(dve.tensor_reduce(s1[:], lz[:], AX.X, ALU.add))
            then(dve.reciprocal(s2[:], s1[:]))
            then(dve.tensor_tensor(pr[:], lz[:], over_experts(s2[:]), ALU.mult))
            for m, oh in ((m1, oh1), (m2, oh2)):
                then(dve.tensor_reduce(m[:], pr[:], AX.X, ALU.max))
                then(dve.tensor_tensor(tmp[:], pr[:], over_experts(m[:]), ALU.is_equal))
                then(dve.tensor_tensor(tmp[:], tmp[:], over_tiles(order[:]), ALU.mult))
                then(dve.tensor_reduce(best[:], tmp[:], AX.X, ALU.min))
                then(dve.tensor_tensor(oh[:], over_tiles(order[:]), over_experts(best[:]), ALU.is_equal))
                if oh is oh1:
                    then(dve.scalar_tensor_tensor(out=pr[:], in0=oh[:], scalar=-4.0, in1=pr[:], op0=ALU.mult, op1=ALU.add))
            then(dve.tensor_tensor(s1[:], m1[:], m2[:], ALU.add))
            then(dve.tensor_scalar(s1[:], s1[:], 1e-9, None, ALU.max))
            then(dve.reciprocal(s2[:], s1[:]))
            dve.tensor_tensor(m1[:], m1[:], s2[:], ALU.mult)
            then(dve.tensor_tensor(m2[:], m2[:], s2[:], ALU.mult))
            then(dve.tensor_tensor(tmp[:], oh1[:], oh2[:], ALU.add))
            for e in range(NE):
                ins = dve.tensor_tensor(elig[:], tmp[:, :, e], nfb[:], ALU.mult)
                ins.then_inc(elig_done, 1)
                dve.wait_ge(counted, e + 1)
                then(dve.tensor_tensor_scan(incl[:], ones[:], pp[:, 1, 0:TT], 0.0, ALU.mult, ALU.add))
                then(dve.tensor_tensor(pos[:], incl[:], pp[:, 1, 0:TT], ALU.subtract))
                then(dve.tensor_tensor(pos[:], pos[:], pp[:, 0, 0:TT], ALU.add))
                then(dve.scalar_tensor_tensor(out=kept[:], in0=pos[:], scalar=float(CAP), in1=elig[:], op0=ALU.is_lt, op1=ALU.mult))
                dve.scalar_tensor_tensor(out=taken[:, :, e], in0=pos[:], scalar=float(e * CAP), in1=kept[:], op0=ALU.add, op1=ALU.mult)
                then(dve.tensor_tensor(over[:], elig[:], kept[:], ALU.subtract))
                then(dve.tensor_tensor(nfb[:], nfb[:], over[:], ALU.subtract))
            dve.tensor_scalar(fbm[:], nfb[:], -1.0, 1.0, ALU.mult, ALU.add).then_inc(away_done, 1)
            dve.wait_ge(counted, NE + 1)
            then(dve.scalar_tensor_tensor(out=incl[:], in0=pp[:, 1, 0:TT], scalar=0.0, in1=to_end[:], op0=ALU.is_gt, op1=ALU.mult))
            then(dve.tensor_reduce(most[:], incl[:], AX.X, ALU.max))
            then(dve.tensor_copy(last_tiles[:], most[:]))
            then(dve.tensor_tensor(token[:], token[:], fbm[:], ALU.mult))
            for k, (m, oh) in enumerate(((m1, oh1), (m2, oh2))):
                then(dve.tensor_tensor(tmp[:], oh[:], taken[:], ALU.mult))
                then(dve.tensor_reduce(best[:], tmp[:], AX.X, ALU.add))
                then(dve.tensor_tensor(best[:], best[:], nfb[:], ALU.mult))
                dve.tensor_tensor(slot_g[:, :, k], best[:], token[:], ALU.add)
                dve.scalar_tensor_tensor(out=slot_s[:, :, k], in0=fbm[:], scalar=float(ROWS), in1=best[:], op0=ALU.mult, op1=ALU.add)
                then(dve.tensor_tensor(wgt[:, :, k], m[:], nfb[:], ALU.mult))
            dve.tensor_tensor(wgt[:, :, 0], wgt[:, :, 0], fbm[:], ALU.add).then_inc(slots_done, 1)

        @block.gpsimd
        def _(pool):
            last_row = pool.to_reg(ROWS - 1)
            pool.wait_ge(slots_done, 1)
            pool.wait_ge(zeroed, 16 * (NZ + NF))
            with pool.Fori(0, TT // NBUF) as m:
                for k in range(NBUF):
                    t = m * NBUF + k
                    pool.wait_ge(scattered[k], m * 32)
                    pool.sem_inc(idx_seen, 1)
                    pool.tensor_copy(idx[:, k:k + 1], slot_s[:, bass.ds(t, 1), :]).then_inc(idx_set, 1)
                    pool.wait_ge(xs_in[k], (m + 1) * 16)
                    pool.wait_ge(idx_set, t + 1)
                    pool.sem_inc(idx_seen, 1)
                    for c in range(TOPK):
                        pool.indirect_dma_start(xg_d, bass.IndirectOffsetOnAxis(idx[:, k, c:c + 1], 0), xs[:, k], None,
                                                bounds_check=last_row, oob_is_err=False).then_inc(scattered[k], 16)
            for k in range(NBUF):
                pool.wait_ge(scattered[k], 32 * (TT // NBUF))


def ffn(nc, a, xg_d, yg_d, ident, last_tiles):
    networks(nc, a, xg_d, yg_d, ident, "f", SLOTS, T // RT // 2, 2, [NE], False, last_tiles)
    networks(nc, a, xg_d, yg_d, ident, "e", 0, NE // 2, 2 * CAP // RT, [0, 1], True)


def networks(nc, a, xg_d, yg_d, ident, tag, row0, loops, body, nets, moving, last_tiles=None):
    def tiles_to_do(engine):
        return None if last_tiles is None else engine.value_load(last_tiles[0:1, 0:1], min_val=0, max_val=TT)

    def where_needed(engine, tiles, m):
        return nullcontext() if tiles is None else engine.If(tiles > m * (body * RT // P))

    with ExitStack() as es:
        def sb(name, shape, dt=F32):
            return es.enter_context(nc.sbuf_tensor(tag + name, shape, dt))

        def sem(name):
            return es.enter_context(nc.semaphore(tag + name))

        NW = len(nets)
        per = body // NW
        KB = RT // P
        w1 = sb("w1", [P, NW, EC, HID])
        w2 = sb("w2", [P, NW, HC, E])
        b1 = sb("b1", [P, NW, HC])
        b2 = sb("b2", [P, NW, E])
        xin = sb("xin", [P, 2, KB, E])
        xt = sb("xt", [P, 2, EC, RT])
        hid = sb("hid", [P, 2, HC, RT])
        yo = sb("yo", [P, 2, KB, E])
        px = es.enter_context(nc.psum_tensor(tag + "px", [P, EC, 512], F32))
        ph = es.enter_context(nc.psum_tensor(tag + "ph", [P, 3, 512], F32))
        py = es.enter_context(nc.psum_tensor(tag + "py", [P, 3, 512], F32))
        w_in = [sem(f"w_in{k}") for k in range(NW)]
        x_in = [sem("x_in0"), sem("x_in1")]
        turned, out0, out1, up_done, act_done, down_done, y_out = (
            sem(n) for n in ("turned", "out0", "out1", "up_done", "act_done", "down_done", "y_out"))
        y_stored = [sem("y_stored0"), sem("y_stored1")]
        stores_seen, weights_free = sem("stores_seen"), sem("weights_free")
        block = es.enter_context(nc.Block())

        def h_bank(y, h):
            return (y * HC + h) % 3

        def y_bank(y, k):
            return (y * KB + k) % 3

        def rows(t, m, y):
            if last_tiles is None:
                first = m * (body * RT) + (row0 + y * RT)
            else:
                first = m * (-body * RT) + ((loops - 1) * body * RT + row0 + y * RT)
            return t[bass.ds(first, RT), :].rearrange("(k p) e -> p k e", p=P)

        @block.sync
        def _(sp):
            tiles = tiles_to_do(sp)

            def load_weights(m, k):
                net = m * 2 + nets[k] if moving else nets[k]
                sp.dma_start(w1[:, k], a["w1"][bass.ds(net, 1)].rearrange("o (c p) n -> p (o c) n", p=P)).then_inc(w_in[k], 16)
                sp.dma_start(w2[:, k], a["w2"][bass.ds(net, 1)].rearrange("o (c p) n -> p (o c) n", p=P)).then_inc(w_in[k], 16)
                sp.dma_start(b1[:, k], a["b1"][bass.ds(net, 1)].rearrange("o p n -> p (o n)")).then_inc(w_in[k], 16)
                sp.dma_start(b2[:, k], a["b2"][bass.ds(net, 1), :].to_broadcast([P, E])).then_inc(w_in[k], 16)

            if not moving:
                load_weights(0, 0)
                sp.wait_ge(w_in[0], 64)
            else:
                load_weights(0, 0)
            with sp.Fori(0, loops) as m:
                with where_needed(sp, tiles, m):
                    for y in range(body):
                        if moving and y == 2:
                            sp.wait_ge(y_out, m * (body * KB))
                            load_weights(m, 1)
                        if moving and y == per + 2:
                            sp.wait_ge(y_out, (m * body + per) * KB)
                            sp.sem_inc(weights_free, 1)
                            with sp.If(m < loops - 1):
                                load_weights(m + 1, 0)
                        if y >= 2:
                            sp.wait_ge(turned, m * body + y - 1)
                        else:
                            sp.wait_ge(turned, m * body)
                        sp.dma_start(xin[:, y % 2], rows(xg_d, m, y)).then_inc(x_in[y % 2], 16)

        @block.gpsimd
        def _(pool):
            tiles = tiles_to_do(pool)
            with pool.Fori(0, loops) as m:
                with where_needed(pool, tiles, m):
                    for y in range(body):
                        pool.wait_ge(y_out, (m * body + y + 1) * KB)
                        pool.dma_start(rows(yg_d, m, y), yo[:, y % 2]).then_inc(y_stored[y % 2], 16)
                    for k in range(2):
                        pool.wait_ge(y_stored[k], (m + 1) * (16 * body // 2))
                    pool.sem_inc(stores_seen, 1)

        @block.tensor
        def _(pe):
            tiles = tiles_to_do(pe)
            with pe.Fori(0, loops) as m:
                with where_needed(pe, tiles, m):
                    def turn(y):
                        n = m * body + y
                        pe.wait_ge(x_in[y % 2], (m * (body // 2) + y // 2 + 1) * 16)
                        pe.wait_ge(out0, n)
                        pe.wait_ge(out1, n)
                        for c in range(EC):
                            for k in range(KB):
                                mm = pe.transpose(px[:, c, k * P:(k + 1) * P], xin[:, y % 2, k, c * P:(c + 1) * P], ident[:])
                        mm.then_inc(turned, 1)

                    def up(y):
                        n, w = m * body + y, y // per
                        if y % per == 0:
                            pe.wait_ge(w_in[w], (m + 1) * 64 if moving else 64)
                        pe.wait_ge(out0, n + 1)
                        pe.wait_ge(out1, n + 1)
                        for h in range(HC):
                            if y > 0 or h >= 3:
                                pe.wait_ge(act_done, n * HC + h - 2)
                            for c in range(EC):
                                mm = pe.matmul(ph[:, h_bank(y, h), :], w1[:, w, c, h * P:(h + 1) * P], xt[:, y % 2, c, :], start=c == 0, stop=c == EC - 1)
                            mm.then_inc(up_done, 1)

                    def down(y):
                        n, w = m * body + y, y // per
                        pe.wait_ge(act_done, (n + 1) * HC)
                        for k in range(KB):
                            if y > 0 or k >= 3:
                                pe.wait_ge(y_out, n * KB + k - 2)
                            for h in range(HC):
                                mm = pe.matmul(py[:, y_bank(y, k), 0:E], hid[:, y % 2, h, k * P:(k + 1) * P], w2[:, w, h, :], start=h == 0, stop=h == HC - 1)
                            mm.then_inc(down_done, 1)

                    turn(0)
                    pe.wait_ge(act_done, m * (body * HC))
                    pe.wait_ge(y_out, m * (body * KB))
                    for y in range(body):
                        up(y)
                        if y + 1 < body:
                            turn(y + 1)
                        down(y)

        @block.scalar
        def _(act):
            tiles = tiles_to_do(act)
            with act.Fori(0, loops) as m:
                with where_needed(act, tiles, m):
                    def out_of_px(y):
                        n = m * body + y
                        act.wait_ge(turned, n + 1)
                        act.wait_ge(up_done, (n - 1) * HC if y >= 1 else n * HC)
                        act.activation(xt[:, y % 2, 1], px[:, 1, :], ACT.Copy).then_inc(out1, 1)

                    out_of_px(0)
                    for y in range(body):
                        n, w = m * body + y, y // per
                        act.wait_ge(down_done, (n - 1) * KB if y >= 1 else n * KB)
                        for h in range(HC):
                            act.wait_ge(up_done, n * HC + h + 1)
                            act.activation(hid[:, y % 2, h, :], ph[:, h_bank(y, h), :], ACT.Gelu, bias=b1[:, w, h:h + 1]).then_inc(act_done, 1)
                        if y + 1 < body:
                            out_of_px(y + 1)

        @block.vector
        def _(dve):
            tiles = tiles_to_do(dve)
            with dve.Fori(0, loops) as m:
                with where_needed(dve, tiles, m):
                    def out_of_px(y):
                        n = m * body + y
                        dve.wait_ge(turned, n + 1)
                        dve.wait_ge(up_done, (n - 1) * HC if y >= 1 else n * HC)
                        dve.tensor_copy(xt[:, y % 2, 0], px[:, 0, :]).then_inc(out0, 1)

                    out_of_px(0)
                    for y in range(body):
                        n, w = m * body + y, y // per
                        if y + 1 < body:
                            out_of_px(y + 1)
                        dve.wait_ge(y_stored[y % 2], (m * (body // 2) + y // 2) * 16)
                        if y % per == 0:
                            dve.wait_ge(w_in[w], (m + 1) * 64 if moving else 64)
                        for k in range(KB):
                            dve.wait_ge(down_done, n * KB + k + 1)
                            dve.tensor_tensor(yo[:, y % 2, k], py[:, y_bank(y, k), 0:E], b2[:, w], ALU.add).then_inc(y_out, 1)


def combine(nc, a, xg_d, yg_d, slot_g, wgt, out):
    with ExitStack() as es:
        def sb(name, shape, dt=F32):
            return es.enter_context(nc.sbuf_tensor(name, shape, dt))

        def sem(name):
            return es.enter_context(nc.semaphore(name))

        def sems(name):
            return [sem(f"{name}{h}") for h in range(2)]

        NBUF = 4
        GP = TT // NBUF // 2
        idx = sb("c_idx", [P, 2, NBUF, TOPK], U32)
        w = sb("c_w", [P, 2, NBUF, TOPK])
        yk = [sb(f"c_y{c}", [P, 2, NBUF, E]) for c in range(TOPK)]
        x1 = sb("c_x1", [P, 2, NBUF, E])
        acc = sb("c_acc", [P, 2, NBUF, E])
        tot = sb("c_tot", [P, 2, NBUF, E])
        stats = sb("c_stats", [P, 2, NBUF, 6])
        mv = sb("c_mv", [P, 2, NBUF, 2])
        std = sb("c_std", [P, 2, NBUF])
        rstd = sb("c_rstd", [P, 2, NBUF])
        eps = sb("c_eps", [P, 1])
        res = sb("c_res", [P, 2, NBUF, E])
        idx_seen, stat_seen, eps_set = sem("c_idx_seen"), sem("c_stat_seen"), sem("c_eps_set")
        gathered = [[sem(f"c_g{h}{k}") for k in range(NBUF)] for h in range(2)]
        x_in, stored = sems("c_x"), sems("c_st")
        idx_set, w_set = sems("c_idx_set"), sems("c_w_set")
        first, added, stat_done, mean_done, std_done, rstd_done, res_done = (
            sems("c_" + n) for n in ("first", "added", "stat_done", "mean_done", "std_done", "rstd_done", "res_done"))
        block = es.enter_context(nc.Block())

        def group(m, h):
            return m * (2 * NBUF) + h * NBUF

        def rows(t, m, h, row0=0):
            return t[bass.ds(m * (2 * NBUF * P) + (h * NBUF * P + row0), NBUF * P), :].rearrange("(k p) e -> p k e", p=P)

        @block.gpsimd
        def _(pool):
            pool.memset(eps[:], EPS).then_inc(eps_set, 1)
            last_row = pool.to_reg(ROWS - 1)
            with pool.Fori(0, GP) as m:
                for h in range(2):
                    pool.wait_ge(added[h], m * NBUF)
                    pool.sem_inc(idx_seen, 1)
                    pool.tensor_copy(idx[:, h], slot_g[:, bass.ds(group(m, h), NBUF), :]).then_inc(idx_set[h], 1)
                    pool.wait_ge(idx_set[h], m + 1)
                    pool.sem_inc(idx_seen, 1)
                    for k in range(NBUF):
                        for c in range(TOPK):
                            pool.indirect_dma_start(yk[c][:, h, k], None, yg_d, bass.IndirectOffsetOnAxis(idx[:, h, k, c:c + 1], 0),
                                                    bounds_check=last_row, oob_is_err=False).then_inc(gathered[h][k], 16)

        @block.sync
        def _(sp):
            with sp.Fori(0, GP) as m:
                for h in range(2):
                    sp.wait_ge(added[h], m * NBUF)
                    sp.dma_start(x1[:, h], rows(xg_d, m, h, SLOTS)).then_inc(x_in[h], 16)

        @block.scalar
        def _(act):
            act.wait_ge(eps_set, 1)
            with act.Fori(0, GP) as m:
                for h in range(2):
                    act.wait_ge(mean_done[h], (m + 1) * NBUF)
                    act.activation(std[:, h], mv[:, h, :, 1], ACT.Sqrt, bias=eps[:, 0:1]).then_inc(std_done[h], 1)
                    act.wait_ge(res_done[h], (m + 1) * NBUF)
                    act.dma_start(rows(out, m, h), res[:, h]).then_inc(stored[h], 16)
            for h in range(2):
                act.wait_ge(stored[h], 16 * GP)

        @block.vector
        def _(dve):
            with dve.Fori(0, GP) as m:
                for h in range(2):
                    dve.tensor_copy(w[:, h], wgt[:, bass.ds(group(m, h), NBUF), :]).then_inc(w_set[h], 1)
                    dve.wait_ge(w_set[h], m + 1)
                    dve.wait_ge(x_in[h], (m + 1) * 16)
                    for k in range(NBUF):
                        dve.wait_ge(gathered[h][k], (m + 1) * 32)
                        dve.scalar_tensor_tensor(out=acc[:, h, k], in0=yk[0][:, h, k], scalar=w[:, h, k, 0:1], in1=x1[:, h, k], op0=ALU.mult, op1=ALU.add).then_inc(first[h], 1)
                    for k in range(NBUF):
                        dve.wait_ge(first[h], m * NBUF + k + 1)
                        dve.scalar_tensor_tensor(out=tot[:, h, k], in0=yk[1][:, h, k], scalar=w[:, h, k, 1:2], in1=acc[:, h, k], op0=ALU.mult, op1=ALU.add).then_inc(added[h], 1)
                    for k in range(NBUF):
                        dve.wait_ge(added[h], m * NBUF + k + 1)
                        dve.bn_stats(stats[:, h, k], tot[:, h, k]).then_inc(stat_done[h], 1)
                    dve.wait_ge(stat_done[h], (m + 1) * NBUF)
                    dve.sem_inc(stat_seen, 1)
                    for k in range(NBUF):
                        dve.bn_aggr(mv[:, h, k], stats[:, h, k]).then_inc(mean_done[h], 1)
                    dve.wait_ge(std_done[h], m + 1)
                    dve.reciprocal(rstd[:, h], std[:, h]).then_inc(rstd_done[h], 1)
                    dve.wait_ge(rstd_done[h], m + 1)
                    dve.wait_ge(stored[h], m * 16)
                    for k in range(NBUF):
                        dve.tensor_scalar(res[:, h, k], tot[:, h, k], mv[:, h, k, 0:1], rstd[:, h, k:k + 1], ALU.subtract, ALU.mult).then_inc(res_done[h], 1)


def laid_out(i):
    i = {k: np.asarray(v) for k, v in i.items()}
    x = i["L0_attn_hidden_states"]
    rep = lambda v: np.broadcast_to(v, (P, *v.shape))
    rel, gc = i["L0_attn_rel_embed"], i["L0_attn_gru_const"].reshape(H)
    stack = lambda e, f: np.concatenate([i[e], i[f][None]])
    a = {
        "x": x.reshape(T, E), "xt": x.transpose(0, 2, 1),
        "wq": i["L0_attn_Wq"].T, "wk": i["L0_attn_Wk"].T, "wv": i["L0_attn_Wv"].T, "wo": i["L0_attn_Wo"].T,
        "bq": i["L0_attn_bq"].reshape(EC, P).T, "bk": i["L0_attn_bk"].reshape(EC, P).T,
        "bv": rep(i["L0_attn_bv"]), "bo": rep(i["L0_attn_bo"]),
        "gru_w": np.tile(i["L0_attn_gru_W"].T, (P // D, 1)).reshape(P, 2, 4),
        "gru_b": rep(i["L0_attn_gru_b"].reshape(2, 4)),
        "gc_hj": np.repeat(gc, NI)[:, None], "gc_h": rep(gc),
        "rel": rel, "ends": rep(rel[[NEG, POS]]),
        "far_ends": np.repeat(rel[[NEG, POS]].T, NI, axis=0),
        "wr": i["L0_ffn_Wr"].T,
        "w1": stack("L0_ffn_W1", "L0_ffn_fw1"), "w2": stack("L0_ffn_W2", "L0_ffn_fw2"),
        "b1": stack("L0_ffn_b1", "L0_ffn_fb1").reshape(NE + 1, HC, P).transpose(0, 2, 1),
        "b2": stack("L0_ffn_b2", "L0_ffn_fb2"),
    }
    return {k: np.ascontiguousarray(v) for k, v in (a | shape_constants()).items()}


def kernel(**inputs):
    import concourse.bacc as _bacc
    from concourse.bass_utils import run_bass_kernel_spmd as _run

    nc = _bacc.Bacc("TRN2", target_bir_lowering=False, num_devices=1)
    arrays, args = {}, {}
    for name, v in laid_out(inputs).items():
        arrays[f"in_{name}"] = v
        args[name] = nc.dram_tensor(f"in_{name}", v.shape, mybir.dt.from_np(v.dtype), kind="ExternalInput").ap()
    out = nc.dram_tensor("out_dram", (T, E), F32, kind="ExternalOutput").ap()
    layer(nc, args, out)
    r = _run(nc, [arrays], core_ids=[0])
    return r.results[0]["out_dram"].reshape(B, N, E)
```
